# Optimizing a Trainium2 kernel written in Bass

```python
import numpy as np
import jax
import jax.numpy as jnp

def _softmax(x, axis=-1):
    return jax.nn.softmax(x, axis=axis)

def _gelu(x):
    return jax.nn.gelu(x, approximate=True)

def _silu(x):
    return jax.nn.silu(x)

def _sigmoid(x):
    return jax.nn.sigmoid(x)

def _layernorm(x, axis=-1, eps=1e-05):
    m = jnp.mean(x, axis=axis, keepdims=True)
    v = jnp.var(x, axis=axis, keepdims=True)
    return (x - m) / jnp.sqrt(v + eps)

def _scatter_add(tgt, idx, src, axis=0):
    return tgt.at[idx].add(src)

def _segment_sum(src, seg, n):
    return jax.ops.segment_sum(src, seg, n)
kernel_name = 'mk_cond_resid_d2_seqx_r8_a81c6f'

def setup_inputs(seed: int=0):
    np.random.seed(seed)
    _w = jnp.asarray

    def _rec_inputs():
        import jax
        import jax.numpy as jnp
        _rk = jax.random.key(seed)
        x = 7.22e-05 + 1 * jax.random.normal(jax.random.fold_in(_rk, 1), (128, 32, 128), jnp.float32)
        _lenS = 32 - jax.random.randint(jax.random.fold_in(_rk, 7), (128,), 0, max(1, 32 // 4) + 1, jnp.int32)
        _lenS2 = 32 - jax.random.randint(jax.random.fold_in(_rk, 8), (128,), 0, max(1, 32 // 4) + 1, jnp.int32)
        cond_8 = -0.104238 + 1.01173 * jax.random.normal(jax.random.fold_in(_rk, 11), (128, 8), jnp.float32)
        return (x, cond_8)
    x, cond_8 = _rec_inputs()

    def _L0_cond_setup():
        import jax, jax.numpy as jnp
        import numpy as np
        TOP_K = 2
        NUM_MOE_LAYERS = 12

        def _gemma_mlp(x, gate_w, up_w, down_w):
            g = jnp.einsum('bsh,hi->bsi', x, gate_w)
            u = jnp.einsum('bsh,hi->bsi', x, up_w)
            return jnp.einsum('bsi,ih->bsh', jax.nn.gelu(g, approximate=True) * u, down_w)
        key = jax.random.key(seed)
        ks = jax.random.split(key, 8)
        B, S, H, I, E = (32, 32, 128, 512, 8)
        std = 0.02
        return {'x': jax.random.normal(ks[0], (B, S, H), jnp.float32), 'router_logits': jax.random.normal(ks[1], (B, E), jnp.float32), 'skill_gate': jax.random.normal(ks[2], (E, H, I), jnp.float32) * std, 'skill_up': jax.random.normal(ks[3], (E, H, I), jnp.float32) * std, 'skill_down': jax.random.normal(ks[4], (E, I, H), jnp.float32) * std, 'shared_gate': jax.random.normal(ks[5], (H, I), jnp.float32) * std, 'shared_up': jax.random.normal(ks[6], (H, I), jnp.float32) * std, 'shared_down': jax.random.normal(ks[7], (I, H), jnp.float32) * std}
    _L0_cond_all = _L0_cond_setup()
    _L0_cond_in = {k: v for k, v in _L0_cond_all.items() if k in ('skill_gate', 'skill_up', 'skill_down', 'shared_gate', 'shared_up', 'shared_down')}
    del _L0_cond_all

    def _L1_cond_setup():
        import jax, jax.numpy as jnp
        import numpy as np
        R = 16
        ALPHA = 32.0
        SCALING = ALPHA / R
        key = jax.random.key(seed)
        ks = jax.random.split(key, 6)
        B, T, C, O, E = (16, 1500, 128, 128, 8)
        x = jax.random.normal(ks[0], (B, T, C), dtype=jnp.float32)
        w = jax.random.uniform(ks[1], (B, E), dtype=jnp.float32)
        W_base = jax.random.normal(ks[2], (O, C), dtype=jnp.float32) * 0.02
        b_base = jax.random.normal(ks[3], (O,), dtype=jnp.float32) * 0.02
        As = jax.random.normal(ks[4], (E, R, C), dtype=jnp.float32) * 0.02
        Bs = jax.random.normal(ks[5], (E, O, R), dtype=jnp.float32) * 0.02
        return {'x': x, 'w': w, 'W_base': W_base, 'b_base': b_base, 'As': As, 'Bs': Bs}
    _L1_cond_all = _L1_cond_setup()
    _L1_cond_in = {k: v for k, v in _L1_cond_all.items() if k in ('W_base', 'b_base', 'As', 'Bs')}
    del _L1_cond_all
    return {'x': x, 'cond_8': cond_8, 'L0_cond_skill_gate': _L0_cond_in['skill_gate'], 'L0_cond_skill_up': _L0_cond_in['skill_up'], 'L0_cond_skill_down': _L0_cond_in['skill_down'], 'L0_cond_shared_gate': _L0_cond_in['shared_gate'], 'L0_cond_shared_up': _L0_cond_in['shared_up'], 'L0_cond_shared_down': _L0_cond_in['shared_down'], 'L1_cond_W_base': _L1_cond_in['W_base'], 'L1_cond_b_base': _L1_cond_in['b_base'], 'L1_cond_As': _L1_cond_in['As'], 'L1_cond_Bs': _L1_cond_in['Bs']}

def reference(x, cond_8, L0_cond_skill_gate, L0_cond_skill_up, L0_cond_skill_down, L0_cond_shared_gate, L0_cond_shared_up, L0_cond_shared_down, L1_cond_W_base, L1_cond_b_base, L1_cond_As, L1_cond_Bs):
    import jax
    import jax.numpy as jnp

    def _L0_cond_ref(x, router_logits, skill_gate, skill_up, skill_down, shared_gate, shared_up, shared_down):
        import jax, jax.numpy as jnp
        import numpy as np
        TOP_K = 2
        NUM_MOE_LAYERS = 12

        def _gemma_mlp(x, gate_w, up_w, down_w):
            g = jnp.einsum('bsh,hi->bsi', x, gate_w)
            u = jnp.einsum('bsh,hi->bsi', x, up_w)
            return jnp.einsum('bsi,ih->bsh', jax.nn.gelu(g, approximate=True) * u, down_w)
        B = x.shape[0]
        E = skill_gate.shape[0]
        rw = jax.nn.softmax(router_logits.astype(jnp.float32), axis=-1)
        w, sel = jax.lax.top_k(rw, TOP_K)
        w = w / w.sum(axis=-1, keepdims=True)
        w = w.astype(x.dtype)
        scale = 1.0 / NUM_MOE_LAYERS
        w = scale * w + (1.0 - scale) * jax.lax.stop_gradient(w)
        dense_w = jnp.zeros((B, E), x.dtype).at[jnp.arange(B)[:, None], sel].add(w)

        def step(acc, params):
            g, u, d, we = params
            return (acc + we[:, None, None] * _gemma_mlp(x, g, u, d), None)
        out, _ = jax.lax.scan(step, jnp.zeros_like(x), (skill_gate, skill_up, skill_down, dense_w.T))
        out = out + _gemma_mlp(x, shared_gate, shared_up, shared_down)
        return out

    def _L1_cond_ref(x, w, W_base, b_base, As, Bs):
        import jax, jax.numpy as jnp
        import numpy as np
        R = 16
        ALPHA = 32.0
        SCALING = ALPHA / R
        out = jnp.einsum('btc,oc->bto', x, W_base) + b_base
        h = jnp.einsum('btc,erc->bter', x, As)
        lora = jnp.einsum('bter,eor,be->bto', h, Bs, w)
        return out + lora * SCALING
    x = x + _L0_cond_ref(x, cond_8, L0_cond_skill_gate, L0_cond_skill_up, L0_cond_skill_down, L0_cond_shared_gate, L0_cond_shared_up, L0_cond_shared_down)
    x = x + _L1_cond_ref(x, cond_8, L1_cond_W_base, L1_cond_b_base, L1_cond_As, L1_cond_Bs)
    return x

_drawn_inputs = setup_inputs


def setup_inputs(seed=0):
    import zlib

    import numpy as np

    out = dict(_drawn_inputs(seed))
    spreads = {}
    factors = {'L0_cond_skill_gate': 6.34,
     'L0_cond_skill_up': 6.284,
     'L0_cond_skill_down': 6.271,
     'L0_cond_shared_gate': 4.733,
     'L0_cond_shared_up': 4.652,
     'L0_cond_shared_down': 4.648,
     'L1_cond_b_base': 9.89}
    for name, (base, spread) in spreads.items():
        noise = np.random.default_rng([zlib.crc32(name.encode()), seed]).standard_normal(out[name].shape)
        drawn = base * np.exp(spread * noise) if base else spread * noise
        out[name] = jnp.asarray(drawn.astype(out[name].dtype))
    for name, factor in factors.items():
        out[name] = (out[name] * factor).astype(out[name].dtype)
    return out
```

```python
from contextlib import ExitStack

import numpy as np

import concourse.bass as bass
from concourse import mybir

P = 128
B, S, H, I = 128, 32, 128, 512
E, K = 8, 2
R, LORA_SCALE = 16, 2.0
NUM_MOE_LAYERS = 12
T = 16
N = T * S
TILES = B // T
UNITS = (K * B + E * (T - 1)) // T
SLOTS = UNITS * T
NB = I // P
FIRST = 2
LAST = TILES - FIRST
ALL = TILES + UNITS
GU = 2 * I
WC = GU + NB * H
CH = WC // NB

C_TRI, C_ID, C_ONE, C_IOTA, C_K16, C_TRI8, C_B, C_END = np.cumsum(
    [0, P, P, P, SLOTS, E, E * E, 1]).tolist()


def constants():
    c = np.zeros((P, C_END), np.float32)
    i = np.arange(P)
    c[:, C_TRI:C_ID] = i[:, None] < i[None, :]
    c[:, C_ID:C_ONE] = np.eye(P)
    c[:, C_ONE:C_IOTA] = 1.0
    c[:, C_IOTA:C_K16] = np.arange(SLOTS)
    c[:, C_K16:C_TRI8] = T * np.arange(E)
    e = np.arange(E)
    c[:, C_TRI8:C_B] = (e[None, :] < e[:, None]).reshape(1, -1)
    c[:, C_B] = i
    return c


def moe_lora_kernel(nc, xT, cond, condT, skill_w, shared_w, lora_w, bias, const, outT):
    f32, f32r = mybir.dt.float32, mybir.dt.float32r
    i32, u32 = mybir.dt.int32, mybir.dt.uint32
    ALU, ACT, AX = mybir.AluOpType, mybir.ActivationFunctionType, mybir.AxisListType
    ENG = mybir.EngineType
    ds = bass.ds

    with ExitStack() as ctx:
        def sb(name, shape, dt=f32):
            return ctx.enter_context(nc.sbuf_tensor(name, shape, dt))

        def bank(name):
            return ctx.enter_context(nc.psum_tensor(name, [P, N], f32))

        def sem(name):
            return ctx.enter_context(nc.semaphore(name))

        acc = sb("acc", [P, B * S])
        x_hl = sb("x_hl", [P, B, 2, S], f32r)
        y = sb("y", [P, SLOTS * S])
        w_raw = [sb(f"w_raw{i}", [P, WC]) for i in range(2)]
        w_hi = [sb(f"w_hi{i}", [P, WC], f32r) for i in range(2)]
        w_lo = [sb(f"w_lo{i}", [P, WC], f32r) for i in range(2)]
        sh_hi = sb("sh_hi", [P, WC], f32r)
        sh_lo = sb("sh_lo", [P, WC], f32r)
        xg = [sb(f"xg{i}", [P, 2, N], f32r) for i in range(2)]
        g = [sb(f"g{i}", [P, N]) for i in range(2)]
        a_hi = [sb(f"a_hi{j}", [P, N], f32r) for j in range(NB)]
        a_lo = [sb(f"a_lo{j}", [P, N], f32r) for j in range(NB)]
        lora_raw = sb("lora_raw", [P, 3 * P])
        lora_hi = sb("lora_hi", [P, 3 * P], f32r)
        lora_lo = sb("lora_lo", [P, 3 * P], f32r)
        bias_sb = sb("bias_sb", [P, 1])
        cond_er = sb("cond_er", [P, B])
        pair = sb("pair", [P, N])
        z_hi = [sb(f"z_hi{i}", [P, N], f32r) for i in range(2)]
        z_lo = [sb(f"z_lo{i}", [P, N], f32r) for i in range(2)]
        h_hi = sb("h_hi", [P, N], f32r)
        h_lo = sb("h_lo", [P, N], f32r)
        out_sb = [sb(f"out_sb{i}", [P, N]) for i in range(2)]
        const_sb = sb("const_sb", [P, C_END])
        logits = sb("logits", [P, E])
        negmax = sb("negmax", [P, 2])
        expd = sb("expd", [P, E])
        expsum = sb("expsum", [P, 2])
        probs = sb("probs", [P, E])
        top = sb("top", [P, 8])
        top_i = sb("top_i", [P, 8], u32)
        top_f = sb("top_f", [P, K])
        hot = sb("hot", [P, K, E])
        chosen = sb("chosen", [P, E])
        topsum = sb("topsum", [P, 2])
        wn = sb("wn", [P, 3, K])
        w_rep = sb("w_rep", [P, K, P])
        more = sb("more", [P, E, E])
        tiles_of = sb("tiles_of", [P, E])
        before = sb("before", [P, E, E])
        start = sb("start", [P, E])
        place = sb("place", [P, E])
        place_k = sb("place_k", [P, K, E])
        pos = sb("pos", [P, K])
        past = sb("past", [1, UNITS, E - 1])
        expert_f = sb("expert_f", [1, UNITS])
        at_slot = sb("at_slot", [P, K + 1, SLOTS])
        w_slot = sb("w_slot", [P, SLOTS])
        expert_i = sb("expert_i", [1, 32], i32)
        slot_i = sb("slot_i", [1, SLOTS], i32)
        pos_i = sb("pos_i", [1, B, K], i32)

        G = [bank("G0"), bank("G1")]
        U = [bank("U0"), bank("U1")]
        D = [bank("D0"), bank("D1")]
        HB, OB = bank("HB"), bank("OB")

        cond_in, const_in = sem("cond_in"), sem("const_in")
        shared_in, x0_in, x_in = sem("shared_in"), sem("x0_in"), sem("x_in")
        lora_in, bias_in, cond_er_in = sem("lora_in"), sem("bias_in"), sem("cond_er_in")
        raw_in = [sem("raw0_in"), sem("raw1_in")]
        negmax_ready, exp_done = sem("negmax_ready"), sem("exp_done")
        chosen_ready, counts_done = sem("chosen_ready"), sem("counts_done")
        expert_ready, slots_ready = sem("expert_ready"), sem("slots_ready")
        tables_done, tables_ready = sem("tables_done"), sem("tables_ready")
        sh_hi_done, sh_lo_done = sem("sh_hi_done"), sem("sh_lo_done")
        x_hi_done, x0_lo_done, x_lo_done = sem("x_hi_done"), sem("x0_lo_done"), sem("x_lo_done")
        lora_hi_done, lora_split = sem("lora_hi_done"), sem("lora_split")
        whi_done, wlo_done, wlo_pool = sem("whi_done"), sem("wlo_done"), sem("wlo_pool")
        gathered = sem("gathered")
        gate_done, up_done, down_done = sem("gate_done"), sem("up_done"), sem("down_done")
        gelu_done, mul_done = sem("gelu_done"), sem("mul_done")
        ahi_done, alo_done = sem("ahi_done"), sem("alo_done")
        y_done = sem("y_done")
        pair_done, z_done = sem("pair_done"), sem("z_done")
        zhi_done, zlo_done = sem("zhi_done"), sem("zlo_done")
        h_done, hw_done = sem("h_done"), sem("hw_done")
        hhi_done, hlo_done = sem("hhi_done"), sem("hlo_done")
        o_done, out_ready = sem("o_done"), sem("out_ready")
        stored = [sem("stored0"), sem("stored1")]
        dve_step = sem("dve_step")

        block = ctx.enter_context(nc.Block())

        def cols(t, n=N):
            return ds(t * n, n)

        def half(r):
            return r // 2 if isinstance(r, int) else r >> 1

        @block.sync
        def _(sp):
            sp.dma_start(logits[:], cond).then_inc(cond_in, 16)
            sp.dma_start(w_raw[1][:], shared_w).then_inc(shared_in, 16)
            sp.dma_start(acc[:, 0:N], xT[:, 0:N]).then_inc(x0_in, 16)
            sp.dma_start(const_sb[:], const).then_inc(const_in, 16)
            sp.dma_start(acc[:, N:], xT[:, N:]).then_inc(x_in, 16)
            sp.dma_start(lora_raw[:], lora_w).then_inc(lora_in, 16)
            sp.dma_start(bias_sb[:], bias).then_inc(bias_in, 16)
            for r in range(R):
                sp.dma_start(cond_er[r:P:R, :], condT).then_inc(cond_er_in, 16)

            def fetch(r, par, reused):
                e = sp.value_load(expert_i[0:1, ds(r, 1)], min_val=0, max_val=E - 1)
                if reused:
                    sp.wait_ge(wlo_done, (NB - 1) * (r - 1))
                    sp.wait_ge(wlo_pool, r - 1)
                sp.dma_start(w_raw[par][:], skill_w[ds(e, 1)].rearrange("e p c -> p (e c)")
                             ).then_inc(raw_in[par], 16)

            sp.wait_ge(expert_ready, 1)
            fetch(0, 0, False)
            sp.wait_ge(sh_hi_done, 1)
            sp.wait_ge(sh_lo_done, 1)
            fetch(1, 1, False)
            with sp.Fori(2, UNITS - 2, 2) as r:
                fetch(r, 0, True)
                fetch(r + 1, 1, True)
            fetch(UNITS - 1, (UNITS - 1) % 2, True)

            for t in range(TILES):
                sp.wait_ge(out_ready, t + 1)
                sp.dma_start(outT[:, t * N:(t + 1) * N], out_sb[t % 2][:]).then_inc(stored[t % 2], 16)
            sp.wait_ge(stored[0], 16 * (TILES // 2))
            sp.wait_ge(stored[1], 16 * (TILES // 2))

        @block.tensor
        def _(pe):
            def product(out, lhs, rhs, start, stop):
                pe.matmul(out, lhs[0], rhs[0], start=start, stop=False)
                pe.matmul(out, lhs[0], rhs[1], start=False, stop=False)
                return pe.matmul(out, lhs[1], rhs[0], start=False, stop=stop)

            def down(v, par, j, w):
                pe.wait_ge(alo_done, NB * v + j + 1)
                c = slice(GU + j * H, GU + (j + 1) * H)
                last = product(D[par][:], (w[0][:, c], w[1][:, c]), (a_hi[j][:], a_lo[j][:]),
                               start=j == 0, stop=j == NB - 1)
                if j == NB - 1:
                    last.then_inc(down_done, 1)

            def unit(v, par, this, before, t=None, lora=None):
                w = (w_hi[par], w_lo[par]) if this == "r" else (sh_hi, sh_lo)
                w_before = (w_hi[1 - par], w_lo[1 - par]) if before == "r" else (sh_hi, sh_lo)
                if this == "r":
                    r = v - FIRST
                    rhs = (xg[par][:, 0, :], xg[par][:, 1, :])
                    pe.wait_ge(gathered, r + 1)
                else:
                    rhs = tuple(x_hl[:, ds(t * T, T), k, :] for k in range(2))
                for j in range(NB):
                    q = NB * v + j
                    first = isinstance(v, int) and q < 2
                    if this == "r":
                        if j < NB - 1:
                            pe.wait_ge(whi_done, NB * r + j + 1)
                            pe.wait_ge(wlo_done, (NB - 1) * r + j + 1)
                        if j == 2:
                            pe.wait_ge(whi_done, NB * r + NB)
                            pe.wait_ge(wlo_pool, r + 1)
                    if not first:
                        pe.wait_ge(gelu_done, q - 1)
                    c = 2 * j * P
                    product(G[j % 2][:], (w[0][:, c:c + P], w[1][:, c:c + P]), rhs, True, True
                            ).then_inc(gate_done, 1)
                    if not first:
                        pe.wait_ge(alo_done, q - 1)
                    c += P
                    product(U[j % 2][:], (w[0][:, c:c + P], w[1][:, c:c + P]), rhs, True, True
                            ).then_inc(up_done, 1)
                    if j < 2:
                        if before is not None:
                            down(v - 1, 1 - par, j + 2, w_before)
                    else:
                        if j == 2 and not (isinstance(v, int) and v < 2):
                            pe.wait_ge(y_done, v - 1)
                        down(v, par, j - 2, w)
                    if lora is not None and j == 1:
                        lora_in_products(lora)
                    if lora is not None and j == 3:
                        lora_out_product(lora)

            lora = [(lora_hi[:, k * P:(k + 1) * P], lora_lo[:, k * P:(k + 1) * P]) for k in range(3)]

            def lora_in_products(t, par=None):
                t, par = t
                z = (z_hi[par][:], z_lo[par][:])
                pe.wait_ge(zlo_done, t + 1)
                if not (isinstance(t, int) and t == 0):
                    pe.wait_ge(hlo_done, t)
                    pe.wait_ge(out_ready, t)
                product(HB[:], lora[0], z, True, True).then_inc(h_done, 1)
                product(OB[:], lora[1], z, True, False)

            def lora_out_product(t):
                t, par = t
                pe.wait_ge(hlo_done, t + 1)
                product(OB[:], lora[2], (h_hi[:], h_lo[:]), False, True).then_inc(o_done, 1)

            pe.wait_ge(const_in, 16)
            pe.wait_ge(chosen_ready, 1)
            pe.matmul(HB[:, 0:E], const_sb[:, C_TRI:C_ID], chosen[:], start=True, stop=True)
            pe.matmul(HB[:, E:2 * E], const_sb[:, C_ONE:C_IOTA], chosen[:], start=True, stop=True
                      ).then_inc(counts_done, 1)

            pe.wait_ge(sh_hi_done, 1)
            pe.wait_ge(sh_lo_done, 1)
            pe.wait_ge(x_hi_done, 1)
            pe.wait_ge(x0_lo_done, 1)
            unit(0, 0, "s", None, t=0)

            pe.wait_ge(slots_ready, 1)
            for k in range(K):
                pe.matmul(OB[:, 0:SLOTS], w_rep[:, k, :], at_slot[:, k, :], start=k == 0, stop=k == K - 1)
            pe.matmul(HB[0:1, 0:SLOTS], const_sb[:, C_B:C_B + 1], at_slot[:, K, :], start=True, stop=True)
            for k in range(K):
                last = pe.matmul(D[1][0:1, k * B:(k + 1) * B], pos[:, k:k + 1], const_sb[:, C_ID:C_ONE],
                                 start=True, stop=True)
            last.then_inc(tables_done, 1)
            pe.wait_ge(x_hi_done, 2)
            pe.wait_ge(x_lo_done, 1)
            pe.wait_ge(tables_ready, 1)
            unit(1, 1, "s", "s", t=1)

            unit(2, 0, "r", "s")
            with pe.Fori(3, 22, 2) as v:
                unit(v, 1, "r", "r")
                unit(v + 1, 0, "r", "r")
            unit(23, 1, "r", "r")
            unit(24, 0, "r", "r")
            unit(25, 1, "s", "r", t=2)
            pe.wait_ge(lora_split, 1)
            unit(26, 0, "s", "s", t=3, lora=(0, 0))
            with pe.Fori(27, 30, 2) as v:
                unit(v, 1, "s", "s", t=v - 23, lora=(v - 26, 1))
                unit(v + 1, 0, "s", "s", t=v - 22, lora=(v - 25, 0))
            down(30, 0, 2, (sh_hi, sh_lo))
            down(30, 0, 3, (sh_hi, sh_lo))
            for t in range(5, TILES):
                lora_in_products((t, t % 2))
                lora_out_product((t, t % 2))

        @block.scalar
        def _(act):
            act.wait_ge(negmax_ready, 1)
            act.activation(expd[:], logits[:], ACT.Exp, bias=negmax[:, 1:2], scale=1.0,
                           accum_out=expsum[:, 0:1]).then_inc(exp_done, 1)
            act.wait_ge(shared_in, 16)
            act.activation(sh_hi[:], w_raw[1][:], ACT.Copy).then_inc(sh_hi_done, 1)
            act.wait_ge(x0_in, 16)
            act.activation(x_hl[:, 0:T, 0, :], acc[:, 0:N].rearrange("p (b s) -> p b s", s=S), ACT.Copy
                           ).then_inc(x_hi_done, 1)
            act.wait_ge(x_in, 16)
            act.activation(x_hl[:, T:, 0, :], acc[:, N:].rearrange("p (b s) -> p b s", s=S), ACT.Copy
                           ).then_inc(x_hi_done, 1)
            act.wait_ge(lora_in, 16)
            act.activation(lora_hi[:], lora_raw[:], ACT.Copy).then_inc(lora_hi_done, 1)

            def unit(v, par, nxt=False, lora=None):
                for j in range(NB):
                    q = NB * v + j
                    first = isinstance(v, int) and q < 2
                    act.wait_ge(gate_done, q + 1)
                    if not first:
                        act.wait_ge(mul_done, q - 1)
                    act.activation(g[j % 2][:], G[j % 2][:], ACT.Gelu_apprx_tanh).then_inc(gelu_done, 1)
                    if nxt:
                        if j == 0:
                            r = v + 1 - FIRST
                            act.wait_ge(raw_in[1 - par], 16 * half(r) + 16)
                        c = slice(j * CH, (j + 1) * CH)
                        act.activation(w_hi[1 - par][:, c], w_raw[1 - par][:, c], ACT.Copy
                                       ).then_inc(whi_done, 1)
                    act.wait_ge(mul_done, q + 1)
                    act.activation(a_hi[j][:], U[j % 2][:], ACT.Copy).then_inc(ahi_done, 1)
                    if lora is not None and j == 0:
                        split_z(*lora)
                    if lora is not None and j == 2:
                        split_h(*lora)

            def split_z(t, par):
                act.wait_ge(z_done, t + 1)
                if not (isinstance(t, int) and t < 2):
                    act.wait_ge(h_done, t - 1)
                    act.wait_ge(o_done, t - 1)
                act.activation(z_hi[par][:], acc[:, cols(t)], ACT.Copy).then_inc(zhi_done, 1)

            def split_h(t, par):
                act.wait_ge(hw_done, t + 1)
                if not (isinstance(t, int) and t == 0):
                    act.wait_ge(o_done, t)
                act.activation(h_hi[:], HB[:], ACT.Copy).then_inc(hhi_done, 1)

            unit(0, 0)
            unit(1, 1, nxt=True)
            unit(2, 0, nxt=True)
            with act.Fori(3, 22, 2) as v:
                unit(v, 1, nxt=True)
                unit(v + 1, 0, nxt=True)
            unit(23, 1, nxt=True)
            unit(24, 0)
            unit(25, 1)
            unit(26, 0, lora=(0, 0))
            with act.Fori(27, 30, 2) as v:
                unit(v, 1, lora=(v - 26, 1))
                unit(v + 1, 0, lora=(v - 25, 0))
            for t in range(5, TILES):
                split_z(t, t % 2)
                split_h(t, t % 2)

        @block.vector
        def _(dve):
            count = [0]

            def then(instruction):
                count[0] += 1
                instruction.then_inc(dve_step, 1)
                dve.wait_ge(dve_step, count[0])

            dve.wait_ge(cond_in, 16)
            then(dve.reduce_max(negmax[:, 0:1], logits[:], AX.X))
            dve.tensor_scalar(negmax[:, 1:2], negmax[:, 0:1], -1.0, None, ALU.mult).then_inc(negmax_ready, 1)
            dve.wait_ge(exp_done, 1)
            then(dve.reciprocal(expsum[:, 1:2], expsum[:, 0:1]))
            then(dve.tensor_scalar(probs[:], expd[:], expsum[:, 1:2], None, ALU.mult))
            then(dve.max(top[:], probs[:]))
            then(dve.max_index(top_i[:], top[:], probs[:]))
            then(dve.tensor_copy(top_f[:], top_i[:, 0:K]))
            dve.wait_ge(const_in, 16)
            dve.tensor_scalar(hot[:, 0, :], const_sb[:, C_IOTA:C_IOTA + E], top_f[:, 0:1], None, ALU.is_equal)
            then(dve.tensor_scalar(hot[:, 1, :], const_sb[:, C_IOTA:C_IOTA + E], top_f[:, 1:2], None, ALU.is_equal))
            dve.tensor_tensor(chosen[:], hot[:, 0, :], hot[:, 1, :], ALU.add).then_inc(chosen_ready, 1)
            dve.wait_ge(sh_hi_done, 1)
            dve.tensor_tensor(sh_lo[:], w_raw[1][:], sh_hi[:].bitcast(f32), ALU.subtract).then_inc(sh_lo_done, 1)
            dve.wait_ge(x_hi_done, 1)
            dve.tensor_tensor(x_hl[:, 0:T, 1, :], acc[:, 0:N].rearrange("p (b s) -> p b s", s=S),
                              x_hl[:, 0:T, 0, :].bitcast(f32), ALU.subtract).then_inc(x0_lo_done, 1)
            then(dve.tensor_tensor(topsum[:, 0:1], top[:, 0:1], top[:, 1:2], ALU.add))
            then(dve.reciprocal(topsum[:, 1:2], topsum[:, 0:1]))
            then(dve.tensor_scalar(wn[:, 0, :], top[:, 0:K], topsum[:, 1:2], None, ALU.mult))
            scale = 1.0 / NUM_MOE_LAYERS
            then(dve.tensor_scalar(wn[:, 1, :], wn[:, 0, :], 1.0 - scale, None, ALU.mult))
            then(dve.scalar_tensor_tensor(wn[:, 2, :], wn[:, 0, :], scale, wn[:, 1, :], ALU.mult, ALU.add))
            dve.tensor_copy(w_rep[:], wn[:, 2, :].unsqueeze(2).to_broadcast([P, K, P]))
            dve.wait_ge(counts_done, 1)
            then(dve.tensor_tensor(more[:], HB[:, E:2 * E].unsqueeze(2).to_broadcast([P, E, E]),
                                   const_sb[:, C_K16:C_TRI8].unsqueeze(1).to_broadcast([P, E, E]), ALU.is_gt))
            then(dve.reduce_sum(tiles_of[:], more[:], AX.X))
            then(dve.tensor_tensor(before[:], const_sb[:, C_TRI8:C_B].rearrange("p (e f) -> p e f", f=E),
                                   tiles_of[:].unsqueeze(1).to_broadcast([P, E, E]), ALU.mult))
            then(dve.reduce_sum(start[:], before[:], AX.X))
            then(dve.tensor_tensor(past[:], const_sb[0:1, C_IOTA:C_IOTA + UNITS].unsqueeze(2).to_broadcast([1, UNITS, E - 1]),
                                   start[0:1, 1:E].unsqueeze(1).to_broadcast([1, UNITS, E - 1]), ALU.is_ge))
            then(dve.reduce_sum(expert_f[:], past[:], AX.X))
            dve.tensor_copy(expert_i[:, 0:UNITS], expert_f[:]).then_inc(expert_ready, 1)
            then(dve.scalar_tensor_tensor(place[:], start[:], float(T), HB[:, 0:E], ALU.mult, ALU.add))
            then(dve.tensor_tensor(place_k[:], hot[:], place[:].unsqueeze(1).to_broadcast([P, K, E]), ALU.mult))
            then(dve.reduce_sum(pos[:], place_k[:], AX.X))
            for k in range(K):
                last = dve.tensor_scalar(at_slot[:, k, :], const_sb[:, C_IOTA:C_K16], pos[:, k:k + 1], None, ALU.is_equal)
            then(last)
            dve.tensor_tensor(at_slot[:, K, :], at_slot[:, 0, :], at_slot[:, 1, :], ALU.add).then_inc(slots_ready, 1)

            def slot_tables():
                dve.wait_ge(tables_done, 1)
                dve.tensor_copy(w_slot[:], OB[:, 0:SLOTS])
                dve.tensor_scalar(slot_i[:], HB[0:1, 0:SLOTS], float(2 * S), None, ALU.mult)
                dve.tensor_scalar(pos_i[:].rearrange("p b k -> p k b"),
                                  D[1][0:1, 0:K * B].rearrange("p (k b) -> p k b", k=K),
                                  float(S), None, ALU.mult).then_inc(tables_ready, 1)

            def unit(v, par, nxt=False, before=None, lora=None, final=None):
                for j in range(NB):
                    q = NB * v + j
                    dve.wait_ge(gelu_done, q + 1)
                    dve.wait_ge(up_done, q + 1)
                    dve.tensor_tensor(U[j % 2][:], g[j % 2][:], U[j % 2][:], ALU.mult).then_inc(mul_done, 1)
                    if nxt and j < NB - 1:
                        dve.wait_ge(whi_done, NB * (v + 1 - FIRST) + j + 1)
                        c = slice(j * CH, (j + 1) * CH)
                        dve.tensor_tensor(w_lo[1 - par][:, c], w_raw[1 - par][:, c],
                                          w_hi[1 - par][:, c].bitcast(f32), ALU.subtract).then_inc(wlo_done, 1)
                    dve.wait_ge(ahi_done, q + 1)
                    dve.tensor_tensor(a_lo[j][:], U[j % 2][:], a_hi[j][:].bitcast(f32), ALU.subtract
                                      ).then_inc(alo_done, 1)
                    if j == 1 and before is not None:
                        finish(v - 1, 1 - par, *before)
                    if lora is not None and j == 0:
                        split_z(*lora)
                    if lora is not None and j == 1:
                        weigh_h(*lora)
                    if lora is not None and j == 2:
                        split_h(*lora)
                    if final is not None and j == 0:
                        output(*final)

            def finish(v, par, kind, t):
                dve.wait_ge(down_done, v + 1)
                if kind == "r":
                    dve.tensor_tensor(y[:, cols(t)].rearrange("p (b s) -> p b s", s=S),
                                      D[par][:].rearrange("p (b s) -> p b s", s=S),
                                      w_slot[:, ds(t * T, T)].unsqueeze(2).to_broadcast([P, T, S]),
                                      ALU.mult).then_inc(y_done, 1)
                else:
                    dve.tensor_tensor(acc[:, cols(t)], D[par][:], acc[:, cols(t)], ALU.add).then_inc(y_done, 1)

            def split_z(t, par):
                dve.wait_ge(zhi_done, t + 1)
                dve.tensor_tensor(z_lo[par][:], acc[:, cols(t)], z_hi[par][:].bitcast(f32), ALU.subtract
                                  ).then_inc(zlo_done, 1)

            def weigh_h(t, par):
                dve.wait_ge(h_done, t + 1)
                dve.tensor_tensor(HB[:].rearrange("p (b s) -> p b s", s=S),
                                  HB[:].rearrange("p (b s) -> p b s", s=S),
                                  cond_er[:, ds(t * T, T)].unsqueeze(2).to_broadcast([P, T, S]),
                                  ALU.mult).then_inc(hw_done, 1)

            def split_h(t, par):
                dve.wait_ge(hhi_done, t + 1)
                dve.tensor_tensor(h_lo[:], HB[:], h_hi[:].bitcast(f32), ALU.subtract).then_inc(hlo_done, 1)

            def output(t, par):
                dve.wait_ge(o_done, t + 1)
                if not (isinstance(t, int) and t < 2):
                    dve.wait_ge(stored[par], 16 * half(t))
                dve.scalar_tensor_tensor(out_sb[par][:], OB[:], bias_sb[:, 0:1], acc[:, cols(t)],
                                         ALU.add, ALU.add).then_inc(out_ready, 1)

            unit(0, 0)
            slot_tables()
            unit(1, 1, nxt=True, before=("s", 0))
            unit(2, 0, nxt=True, before=("s", 1))
            dve.wait_ge(lora_hi_done, 1)
            dve.tensor_tensor(lora_lo[:], lora_raw[:], lora_hi[:].bitcast(f32), ALU.subtract).then_inc(lora_split, 1)
            dve.wait_ge(cond_er_in, 16 * R)
            dve.wait_ge(bias_in, 16)
            then(dve.tensor_scalar(cond_er[:], cond_er[:], LORA_SCALE, None, ALU.mult))
            with dve.Fori(3, 22, 2) as v:
                unit(v, 1, nxt=True, before=("r", v - 3))
                unit(v + 1, 0, nxt=True, before=("r", v - 2))
            unit(23, 1, nxt=True, before=("r", 20))
            unit(24, 0, before=("r", 21))
            unit(25, 1, before=("r", 22))
            unit(26, 0, before=("s", 2), lora=(0, 0))
            with dve.Fori(27, 30, 2) as v:
                unit(v, 1, before=("s", v - 24), lora=(v - 26, 1), final=(v - 27, 0))
                unit(v + 1, 0, before=("s", v - 23), lora=(v - 25, 0), final=(v - 26, 1))
            finish(30, 0, "s", 7)
            output(4, 0)
            for t in range(5, TILES):
                split_z(t, t % 2)
                weigh_h(t, t % 2)
                split_h(t, t % 2)
                output(t, t % 2)

        @block.gpsimd
        def _(pool):
            pool.wait_ge(x_hi_done, 2)
            pool.tensor_tensor(x_hl[:, T:, 1, :], acc[:, N:].rearrange("p (b s) -> p b s", s=S),
                               x_hl[:, T:, 0, :].bitcast(f32), ALU.subtract).then_inc(x_lo_done, 1)
            pool.wait_ge(tables_ready, 1)
            pool.wait_ge(x0_lo_done, 1)
            pool.wait_ge(x_lo_done, 1)

            def prepare(r, par, early=False):
                if not early:
                    pool.wait_ge(up_done, NB * (r + FIRST - 1))
                _, rows = nc.values_load_multi_w_load_instructions(
                    slot_i[0:1, ds(r * T, T)], engines=[ENG.Pool], min_val=0, max_val=(B - 1) * 2 * S,
                    skip_runtime_bounds_check_because="the slots hold 64 times a batch row's number")
                flat = x_hl[:].rearrange("p b k s -> p (b k s)")
                for i in range(T):
                    last = pool.tensor_copy(xg[par][:, :, i * S:(i + 1) * S],
                                            flat[:, ds(rows[i], 2 * S)].rearrange("p (k s) -> p k s", s=S))
                last.then_inc(gathered, 1)
                if not early:
                    pool.wait_ge(down_done, r + FIRST - 1)
                pool.wait_ge(whi_done, NB * r + NB)
                c = slice((NB - 1) * CH, WC)
                pool.tensor_tensor(w_lo[par][:, c], w_raw[par][:, c], w_hi[par][:, c].bitcast(f32),
                                   ALU.subtract).then_inc(wlo_pool, 1)

            prepare(0, 0, early=True)
            prepare(1, 1, early=True)
            with pool.Fori(2, UNITS - 2, 2) as r:
                prepare(r, 0)
                prepare(r + 1, 1)
            prepare(UNITS - 1, (UNITS - 1) % 2)

            def combine(t):
                pool.wait_ge(y_done, max(FIRST + UNITS, UNITS + t + 1))
                for h in range(2):
                    n = T // 2
                    _, at = nc.values_load_multi_w_load_instructions(
                        pos_i[:].rearrange("p b k -> p (b k)")[0:1, t * T * K + h * T:t * T * K + h * T + T],
                        engines=[ENG.Pool], min_val=0, max_val=(SLOTS - 1) * S,
                        skip_runtime_bounds_check_because="the positions are 32 times a slot's number")
                    for i in range(n):
                        c = (h * n + i) * S
                        last = pool.tensor_tensor(pair[:, c:c + S], y[:, ds(at[2 * i], S)],
                                                  y[:, ds(at[2 * i + 1], S)], ALU.add)
                last.then_inc(pair_done, 1)
                pool.wait_ge(pair_done, t + 1)
                pool.tensor_tensor(acc[:, t * N:(t + 1) * N], acc[:, t * N:(t + 1) * N], pair[:], ALU.add
                                   ).then_inc(z_done, 1)
                pool.wait_ge(z_done, t + 1)

            for t in range(TILES):
                combine(t)


_OUT = "out_dram"


def kernel(**inputs):
    import concourse.bacc as bacc
    from concourse.bass_utils import run_bass_kernel_spmd

    x = np.asarray(inputs["x"])
    cond = np.asarray(inputs["cond_8"])

    def packed(gate, up, down):
        lead = gate.shape[:-2]
        gate = gate.reshape(*lead, H, NB, 1, P)
        up = up.reshape(*lead, H, NB, 1, P)
        both = np.concatenate([gate, up], axis=-2).reshape(*lead, H, GU)
        down = np.moveaxis(down.reshape(*lead, NB, P, H), -3, -2).reshape(*lead, P, NB * H)
        return np.ascontiguousarray(np.concatenate([both, down], axis=-1))

    a = {n: np.asarray(v) for n, v in inputs.items()}
    arrays = {
        "xT": np.ascontiguousarray(x.reshape(B * S, H).T),
        "cond": np.ascontiguousarray(cond),
        "condT": np.ascontiguousarray(cond.T),
        "skill_w": packed(a["L0_cond_skill_gate"], a["L0_cond_skill_up"], a["L0_cond_skill_down"]),
        "shared_w": packed(a["L0_cond_shared_gate"], a["L0_cond_shared_up"], a["L0_cond_shared_down"]),
        "lora_w": np.ascontiguousarray(np.concatenate([
            a["L1_cond_As"].reshape(E * R, H).T,
            a["L1_cond_W_base"].T,
            a["L1_cond_Bs"].transpose(0, 2, 1).reshape(E * R, H)], axis=1)),
        "bias": np.ascontiguousarray(a["L1_cond_b_base"].reshape(H, 1)),
        "const": constants(),
    }
    nc = bacc.Bacc("TRN2", target_bir_lowering=False, num_devices=1)
    aps = {n: nc.dram_tensor(n, v.shape, mybir.dt.from_np(v.dtype), kind="ExternalInput").ap()
           for n, v in arrays.items()}
    outT = nc.dram_tensor(_OUT, (H, B * S), mybir.dt.float32, kind="ExternalOutput").ap()
    moe_lora_kernel(nc, **aps, outT=outT)
    result = run_bass_kernel_spmd(nc, [arrays], core_ids=[0]).results[0][_OUT]
    return np.ascontiguousarray(np.asarray(result).T).reshape(B, S, H)
```

```python
from contextlib import ExitStack

import numpy as np

import concourse.bass as bass
from concourse import mybir

P = 128
B, S, H, I = 128, 32, 128, 512
E, K = 8, 2
R, LORA_SCALE = 16, 2.0
NUM_MOE_LAYERS = 12
T = 16
N = T * S
TILES = B // T
UNITS = (K * B + E * (T - 1)) // T
SLOTS = UNITS * T
NB = I // P
FIRST = 2
LAST = TILES - FIRST
ALL = TILES + UNITS
GU = 2 * I
WC = GU + NB * H
X_EARLY = 3
NC = 3
CH = WC // NC

C_TRI, C_ID, C_ONE, C_IOTA, C_K16, C_TRI8, C_B, C_END = np.cumsum(
    [0, P, P, P, SLOTS, E, E * E, 1]).tolist()


def constants():
    c = np.zeros((P, C_END), np.float32)
    i = np.arange(P)
    c[:, C_TRI:C_ID] = i[:, None] < i[None, :]
    c[:, C_ID:C_ONE] = np.eye(P)
    c[:, C_ONE:C_IOTA] = 1.0
    c[:, C_IOTA:C_K16] = np.arange(SLOTS)
    c[:, C_K16:C_TRI8] = T * np.arange(E)
    e = np.arange(E)
    c[:, C_TRI8:C_B] = (e[None, :] < e[:, None]).reshape(1, -1)
    c[:, C_B] = i
    return c


def moe_lora_kernel(nc, xT, cond, condT, skill_w, shared_w, lora_w, bias, const, outT):
    f32, f32r = mybir.dt.float32, mybir.dt.float32r
    i32, u32 = mybir.dt.int32, mybir.dt.uint32
    ALU, ACT, AX = mybir.AluOpType, mybir.ActivationFunctionType, mybir.AxisListType
    ENG = mybir.EngineType
    ds = bass.ds

    with ExitStack() as ctx:
        def sb(name, shape, dt=f32):
            return ctx.enter_context(nc.sbuf_tensor(name, shape, dt))

        def bank(name):
            return ctx.enter_context(nc.psum_tensor(name, [P, N], f32))

        def sem(name):
            return ctx.enter_context(nc.semaphore(name))

        acc = sb("acc", [P, B * S])
        x_hl = sb("x_hl", [P, B, 2, S], f32r)
        y = sb("y", [P, SLOTS * S])
        w_raw = [sb(f"w_raw{i}", [P, WC]) for i in range(2)]
        w_hi = [sb(f"w_hi{i}", [P, WC], f32r) for i in range(2)]
        w_lo = [sb(f"w_lo{i}", [P, WC], f32r) for i in range(2)]
        sh_hi = sb("sh_hi", [P, WC], f32r)
        sh_lo = sb("sh_lo", [P, WC], f32r)
        xg = [sb(f"xg{i}", [P, 2, N], f32r) for i in range(2)]
        g = [sb(f"g{i}", [P, N]) for i in range(2)]
        a_hi = [sb(f"a_hi{j}", [P, N], f32r) for j in range(NB)]
        a_lo = [sb(f"a_lo{j}", [P, N], f32r) for j in range(NB)]
        lora_raw = sb("lora_raw", [P, 3 * P])
        lora_hi = sb("lora_hi", [P, 3 * P], f32r)
        lora_lo = sb("lora_lo", [P, 3 * P], f32r)
        bias_sb = sb("bias_sb", [P, 1])
        cond_er = sb("cond_er", [P, B])
        z_hi = [sb(f"z_hi{i}", [P, N], f32r) for i in range(2)]
        z_lo = [sb(f"z_lo{i}", [P, N], f32r) for i in range(2)]
        h_hi = sb("h_hi", [P, N], f32r)
        h_lo = sb("h_lo", [P, N], f32r)
        pair, *out_sb = (w_raw[0][:, i * N:(i + 1) * N] for i in range(3))
        const_sb = sb("const_sb", [P, C_END])
        logits = sb("logits", [P, E])
        negmax = sb("negmax", [P, 2])
        expd = sb("expd", [P, E])
        expsum = sb("expsum", [P, 2])
        probs = sb("probs", [P, E])
        top = sb("top", [P, 8])
        top_i = sb("top_i", [P, 8], u32)
        top_f = sb("top_f", [P, K])
        hot = sb("hot", [P, K, E])
        chosen = sb("chosen", [P, E])
        topsum = sb("topsum", [P, 2])
        wn = sb("wn", [P, 3, K])
        w_rep = sb("w_rep", [P, 2, K, P], f32r)
        b_rep = sb("b_rep", [P, P], f32r)
        pos_rep = sb("pos_rep", [P, K, P], f32r)
        ident = sb("ident", [P, P], f32r)
        more = sb("more", [P, E, E])
        tiles_of = sb("tiles_of", [P, E])
        before = sb("before", [P, E, E])
        start = sb("start", [P, E])
        place = sb("place", [P, E])
        place_k = sb("place_k", [P, K, E])
        pos = sb("pos", [P, K])
        past = sb("past", [1, UNITS, E - 1])
        expert_f = sb("expert_f", [1, UNITS])
        at_slot = sb("at_slot", [P, K, SLOTS], f32r)
        w_slot = sb("w_slot", [P, SLOTS])
        expert_i = sb("expert_i", [1, 32], i32)
        slot_i = sb("slot_i", [1, SLOTS], i32)
        pos_i = sb("pos_i", [1, B, K], i32)

        G = [bank("G0"), bank("G1")]
        U = [bank("U0"), bank("U1")]
        D = [bank("D0"), bank("D1")]
        HB, OB = bank("HB"), bank("OB")

        cond_in, const_in = sem("cond_in"), sem("const_in")
        shared_in, x0_in = sem("shared_in"), sem("x0_in")
        shared_down_in = sem("shared_down_in")
        x_in = [sem(f"x{t}_in") for t in range(1, TILES)]
        lora_in, bias_in, cond_er_in = sem("lora_in"), sem("bias_in"), sem("cond_er_in")
        raw_in = [sem("raw0_in"), sem("raw1_in")]
        negmax_ready, exp_done = sem("negmax_ready"), sem("exp_done")
        chosen_ready, counts_done = sem("chosen_ready"), sem("counts_done")
        rep_ready = sem("rep_ready")
        expert_ready, slots_ready = sem("expert_ready"), sem("slots_ready")
        tables_done, tables_ready = sem("tables_done"), sem("tables_ready")
        sh_hi_done, sh_lo_done = sem("sh_hi_done"), sem("sh_lo_done")
        x_hi_done, x0_lo_done, x_lo_done = sem("x_hi_done"), sem("x0_lo_done"), sem("x_lo_done")
        lora_ready, lora_hi_done, lora_split = sem("lora_ready"), sem("lora_hi_done"), sem("lora_split")
        whi_done, wlo_done = sem("whi_done"), sem("wlo_done")
        gathered = sem("gathered")
        gate_done, up_done, down_done = sem("gate_done"), sem("up_done"), sem("down_done")
        gelu_done, mul_done = sem("gelu_done"), sem("mul_done")
        ahi_done, alo_done = sem("ahi_done"), sem("alo_done")
        y_done = sem("y_done")
        pair_done, pairs_added = sem("pair_done"), sem("pairs_added")
        zhi_done, zlo_done = sem("zhi_done"), sem("zlo_done")
        h_done, hw_done = sem("h_done"), sem("hw_done")
        hhi_done, hlo_done = sem("hhi_done"), sem("hlo_done")
        o_done, out_ready = sem("o_done"), sem("out_ready")
        stored = [sem("stored0"), sem("stored1")]
        dve_step = sem("dve_step")

        block = ctx.enter_context(nc.Block())

        LORA_ORDER = [*range(FIRST, TILES - 1), 0, 1, TILES - 1]
        TAIL = {
            5: ((xg[0][:, 0, :], xg[0][:, 1, :]), G, (a_hi[0][:], a_lo[0][:])),
            6: ((xg[1][:, 0, :], xg[1][:, 1, :]), U, (a_hi[1][:], a_lo[1][:])),
            7: ((z_hi[1][:], z_lo[1][:]), (D[1], D[0]), (a_hi[2][:], a_lo[2][:])),
        }

        def cols(t, n=N):
            return ds(t * n, n)

        def half(r):
            return r // 2 if isinstance(r, int) else r >> 1

        @block.sync
        def _(sp):
            sp.dma_start(logits[:], cond).then_inc(cond_in, 16)
            sp.dma_start(const_sb[:], const).then_inc(const_in, 16)
            sp.dma_start(w_raw[1][:, 0:GU], shared_w[:, 0:GU]).then_inc(shared_in, 16)
            sp.dma_start(acc[:, 0:N], xT[:, 0:N]).then_inc(x0_in, 16)
            sp.dma_start(w_raw[1][:, GU:], shared_w[:, GU:]).then_inc(shared_down_in, 16)
            for t in range(1, TILES):
                sp.dma_start(acc[:, t * N:(t + 1) * N], xT[:, t * N:(t + 1) * N]).then_inc(x_in[t - 1], 16)

            def fetch(r, par, reused):
                e = sp.value_load(expert_i[0:1, ds(r, 1)], min_val=0, max_val=E - 1)
                if reused:
                    sp.wait_ge(wlo_done, NC * (r - 1))
                sp.dma_start(w_raw[par][:], skill_w[ds(e, 1)].rearrange("e p c -> p (e c)")
                             ).then_inc(raw_in[par], 16)

            sp.wait_ge(expert_ready, 1)
            fetch(0, 0, False)
            sp.wait_ge(sh_hi_done, NC)
            sp.wait_ge(sh_lo_done, NC)
            fetch(1, 1, False)
            sp.dma_start(lora_raw[:], lora_w).then_inc(lora_in, 16)
            sp.dma_start(bias_sb[:], bias).then_inc(bias_in, 16)
            for r in range(R):
                sp.dma_start(cond_er[r:P:R, :], condT).then_inc(cond_er_in, 16)
            with sp.Fori(2, UNITS - 2, 2) as r:
                fetch(r, 0, True)
                fetch(r + 1, 1, True)
            fetch(UNITS - 1, (UNITS - 1) % 2, True)

            for n, t in enumerate(LORA_ORDER):
                sp.wait_ge(out_ready, n + 1)
                sp.dma_start(outT[:, t * N:(t + 1) * N], out_sb[n % 2]).then_inc(stored[n % 2], 16)
            sp.wait_ge(stored[0], 16 * (TILES // 2))
            sp.wait_ge(stored[1], 16 * (TILES // 2))

        @block.tensor
        def _(pe):
            def product(out, lhs, rhs, start, stop):
                pe.matmul(out, lhs[0], rhs[0], start=start, stop=False)
                pe.matmul(out, lhs[0], rhs[1], start=False, stop=False)
                return pe.matmul(out, lhs[1], rhs[0], start=False, stop=stop)

            def down(v, par, j, w):
                pe.wait_ge(alo_done, NB * v + j + 1)
                c = slice(GU + j * H, GU + (j + 1) * H)
                last = product(D[par][:], (w[0][:, c], w[1][:, c]), (a_hi[j][:], a_lo[j][:]),
                               start=j == 0, stop=j == NB - 1)
                if j == NB - 1:
                    last.then_inc(down_done, 1)

            def unit(v, par, this, before, t=None, after_step=()):
                w = (w_hi[par], w_lo[par]) if this == "r" else (sh_hi, sh_lo)
                w_before = (w_hi[1 - par], w_lo[1 - par]) if before == "r" else (sh_hi, sh_lo)
                if this == "r":
                    r = v - FIRST
                    rhs = (xg[par][:, 0, :], xg[par][:, 1, :])
                    pe.wait_ge(gathered, r + 1)
                else:
                    rhs = tuple(x_hl[:, ds(t * T, T), k, :] for k in range(2))
                for j in range(NB):
                    q = NB * v + j
                    first = isinstance(v, int) and q < 2
                    if j % 2 == 0 and this == "r":
                        pe.wait_ge(wlo_done, NC * r + (1 if j == 0 else NC))
                    if j % 2 == 0 and isinstance(v, int) and v == 0:
                        pe.wait_ge(sh_lo_done, 1 if j == 0 else NC)
                    if not first:
                        pe.wait_ge(gelu_done, q - 1)
                    c = 2 * j * P
                    product(G[j % 2][:], (w[0][:, c:c + P], w[1][:, c:c + P]), rhs, True, True
                            ).then_inc(gate_done, 1)
                    if not first:
                        pe.wait_ge(alo_done, q - 1)
                    c += P
                    product(U[j % 2][:], (w[0][:, c:c + P], w[1][:, c:c + P]), rhs, True, True
                            ).then_inc(up_done, 1)
                    if j < 2:
                        if before is not None:
                            down(v - 1, 1 - par, j + 2, w_before)
                    else:
                        if j == 2 and not (isinstance(v, int) and v < 2):
                            pe.wait_ge(y_done, v - 1)
                        down(v, par, j - 2, w)
                    for k, f, args in after_step:
                        if k == j:
                            f(*args)

            lora = [(lora_hi[:, k * P:(k + 1) * P], lora_lo[:, k * P:(k + 1) * P]) for k in range(3)]

            def lora_in_products(n, z, banks, reused=False):
                pe.wait_ge(zlo_done, n + 1)
                if reused:
                    pe.wait_ge(hlo_done, n)
                    pe.wait_ge(out_ready, n)
                product(banks[0][:], lora[0], z, True, True).then_inc(h_done, 1)
                product(banks[1][:], lora[1], z, True, False)

            def lora_out_product(n, h, banks):
                pe.wait_ge(hlo_done, n + 1)
                product(banks[1][:], lora[2], h, False, True).then_inc(o_done, 1)

            pe.wait_ge(const_in, 16)
            pe.wait_ge(chosen_ready, 1)
            pe.matmul(HB[:, 0:E], const_sb[:, C_TRI:C_ID], chosen[:], start=True, stop=True)
            pe.matmul(HB[:, E:2 * E], const_sb[:, C_ONE:C_IOTA], chosen[:], start=True, stop=True
                      ).then_inc(counts_done, 1)

            def table_products():
                pe.wait_ge(slots_ready, 1)
                pe.wait_ge(rep_ready, 2)
                for k in range(K):
                    for part in range(2):
                        pe.matmul(OB[:, 0:SLOTS], w_rep[:, part, k, :], at_slot[:, k, :],
                                  start=k + part == 0, stop=k + part == K)
                for k in range(K):
                    pe.matmul(HB[:, 0:SLOTS], b_rep[:], at_slot[:, k, :], start=k == 0, stop=k == K - 1)
                for k in range(K):
                    last = pe.matmul(D[1][:, k * B:(k + 1) * B], pos_rep[:, k, :], ident[:],
                                     start=True, stop=True)
                last.then_inc(tables_done, 1)

            pe.wait_ge(x_hi_done, 1)
            pe.wait_ge(x0_lo_done, 1)
            unit(0, 0, "s", None, t=0, after_step=[(2, table_products, ())])
            pe.wait_ge(x_hi_done, 2)
            pe.wait_ge(x_lo_done, 1)
            pe.wait_ge(tables_ready, 1)
            unit(1, 1, "s", "s", t=1)
            unit(2, 0, "r", "s")
            with pe.Fori(3, 22, 2) as v:
                unit(v, 1, "r", "r")
                unit(v + 1, 0, "r", "r")
            unit(23, 1, "r", "r")
            unit(24, 0, "r", "r")
            unit(25, 1, "s", "r", t=2)

            def lora_steps(v, par, start=False):
                n = v - 26
                steps = [(3, lora_in_products, (n, z_parts(par), (HB, OB), not start))]
                if not start:
                    steps.append((1, lora_out_product, (n - 1, (h_hi[:], h_lo[:]), (HB, OB))))
                return steps

            def z_parts(par):
                return z_hi[par][:], z_lo[par][:]

            pe.wait_ge(lora_split, 1)
            unit(26, 0, "s", "s", t=3, after_step=lora_steps(26, 0, start=True))
            with pe.Fori(27, 28, 2) as v:
                unit(v, 1, "s", "s", t=v - 23, after_step=lora_steps(v, 1))
                unit(v + 1, 0, "s", "s", t=v - 22, after_step=lora_steps(v + 1, 0))
            unit(29, 1, "s", "s", t=6, after_step=lora_steps(29, 1))
            unit(30, 0, "s", "s", t=7, after_step=lora_steps(30, 0))
            down(30, 0, 2, (sh_hi, sh_lo))
            pe.wait_ge(gelu_done, NB * ALL)
            lora_in_products(5, *TAIL[5][0:2])
            down(30, 0, 3, (sh_hi, sh_lo))
            lora_in_products(6, *TAIL[6][0:2])
            lora_out_product(4, (h_hi[:], h_lo[:]), (HB, OB))
            lora_in_products(7, *TAIL[7][0:2])
            lora_out_product(5, TAIL[5][2], TAIL[5][1])
            lora_out_product(6, TAIL[6][2], TAIL[6][1])
            lora_out_product(7, TAIL[7][2], TAIL[7][1])

        @block.scalar
        def _(act):
            act.wait_ge(negmax_ready, 1)
            act.activation(expd[:], logits[:], ACT.Exp, bias=negmax[:, 1:2], scale=1.0,
                           accum_out=expsum[:, 0:1]).then_inc(exp_done, 1)

            def split_x(t):
                act.wait_ge(x0_in if t == 0 else x_in[t - 1], 16)
                act.activation(x_hl[:, t * T:(t + 1) * T, 0, :],
                               acc[:, t * N:(t + 1) * N].rearrange("p (b s) -> p b s", s=S), ACT.Copy
                               ).then_inc(x_hi_done, 1)

            for k in range(NC):
                act.wait_ge(shared_down_in if k == NC - 1 else shared_in, 16)
                c = slice(k * CH, (k + 1) * CH)
                act.activation(sh_hi[:, c], w_raw[1][:, c], ACT.Copy).then_inc(sh_hi_done, 1)
                if k == 0:
                    split_x(0)
            for t in range(1, X_EARLY):
                split_x(t)

            def unit(v, par, nxt=False, between=(), after_step=()):
                for j in range(NB):
                    q = NB * v + j
                    first = isinstance(v, int) and q < 2
                    act.wait_ge(gate_done, q + 1)
                    if not first:
                        act.wait_ge(mul_done, q - 1)
                    act.activation(g[j % 2][:], G[j % 2][:], ACT.Gelu_apprx_tanh).then_inc(gelu_done, 1)
                    if nxt and j < NC:
                        if j == 0:
                            r = v + 1 - FIRST
                            act.wait_ge(raw_in[1 - par], 16 * half(r) + 16)
                        c = slice(j * CH, (j + 1) * CH)
                        act.activation(w_hi[1 - par][:, c], w_raw[1 - par][:, c], ACT.Copy
                                       ).then_inc(whi_done, 1)
                    for k, f, args in between:
                        if k == j:
                            f(*args)
                    act.wait_ge(mul_done, q + 1)
                    act.activation(a_hi[j][:], U[j % 2][:], ACT.Copy).then_inc(ahi_done, 1)
                    for k, f, args in after_step:
                        if k == j:
                            f(*args)

            def split_z(n, t, out, reused=False):
                if isinstance(t, int) and t < FIRST:
                    act.wait_ge(pairs_added, LAST + t)
                else:
                    act.wait_ge(y_done, t + UNITS + 1)
                if reused:
                    act.wait_ge(o_done, n - 1)
                act.activation(out, acc[:, cols(t)], ACT.Copy).then_inc(zhi_done, 1)

            def split_h(n, out, h_bank, reused=False):
                act.wait_ge(hw_done, n + 1)
                if reused:
                    act.wait_ge(o_done, n)
                act.activation(out, h_bank[:], ACT.Copy).then_inc(hhi_done, 1)

            def output(n, par, o_bank, reused=True):
                act.wait_ge(o_done, n + 1)
                if reused:
                    act.wait_ge(stored[par], 16 * half(n))
                act.activation(out_sb[par], o_bank[:], ACT.Identity, bias=bias_sb[:, 0:1], scale=1.0
                               ).then_inc(out_ready, 1)

            def lora_steps(v, par):
                n = v - 26
                between = []
                if n > 0:
                    between = [(0, split_h, (n - 1, h_hi[:], HB, n > 1)),
                               (2, output, (n - 1, 1 - par, OB, n > 2))]
                return dict(between=between,
                            after_step=[(1, split_z, (n, v - 24, z_hi[par][:], n > 1))])

            unit(0, 0, after_step=[(j, split_x, (X_EARLY + j,)) for j in range(NB)])
            for t in range(X_EARLY + NB, TILES):
                split_x(t)
            unit(1, 1, nxt=True)
            unit(2, 0, nxt=True)
            with act.Fori(3, 22, 2) as v:
                unit(v, 1, nxt=True)
                unit(v + 1, 0, nxt=True)
            unit(23, 1, nxt=True)
            act.wait_ge(lora_ready, 1)
            act.activation(lora_hi[:], lora_raw[:], ACT.Copy).then_inc(lora_hi_done, 1)
            unit(24, 0)
            unit(25, 1)
            act.wait_ge(bias_in, 16)
            for v in range(26, 30):
                unit(v, v % 2, **lora_steps(v, v % 2))
            last = lora_steps(30, 0)
            last["after_step"] += [(2, split_z, (5, 0, TAIL[5][0][0])), (3, split_z, (6, 1, TAIL[6][0][0]))]
            unit(30, 0, **last)
            split_h(4, h_hi[:], HB, True)
            split_z(7, 7, TAIL[7][0][0])
            split_h(5, TAIL[5][2][0], TAIL[5][1][0])
            split_h(6, TAIL[6][2][0], TAIL[6][1][0])
            output(4, 0, OB)
            split_h(7, TAIL[7][2][0], TAIL[7][1][0])
            for n in (5, 6, 7):
                output(n, n % 2, TAIL[n][1][1])

        @block.vector
        def _(dve):
            count = [0]

            def step(instruction):
                count[0] += 1
                instruction.then_inc(dve_step, 1)
                return count[0]

            def seen(n):
                dve.wait_ge(dve_step, n)

            dve.wait_ge(cond_in, 16)
            seen(step(dve.reduce_max(negmax[:, 0:1], logits[:], AX.X)))
            dve.tensor_scalar(negmax[:, 1:2], negmax[:, 0:1], -1.0, None, ALU.mult).then_inc(negmax_ready, 1)
            dve.wait_ge(exp_done, 1)
            seen(step(dve.reciprocal(expsum[:, 1:2], expsum[:, 0:1])))
            seen(step(dve.tensor_scalar(probs[:], expd[:], expsum[:, 1:2], None, ALU.mult)))
            seen(step(dve.max(top[:], probs[:])))
            found = step(dve.max_index(top_i[:], top[:], probs[:]))
            summed = step(dve.tensor_tensor(topsum[:, 0:1], top[:, 0:1], top[:, 1:2], ALU.add))
            seen(found)
            index = step(dve.tensor_copy(top_f[:], top_i[:, 0:K]))
            seen(summed)
            inverted = step(dve.reciprocal(topsum[:, 1:2], topsum[:, 0:1]))
            dve.wait_ge(const_in, 16)
            seen(index)
            marked = step(dve.tensor_tensor(
                hot[:], const_sb[:, C_IOTA:C_IOTA + E].unsqueeze(1).to_broadcast([P, K, E]),
                top_f[:].unsqueeze(2).to_broadcast([P, K, E]), ALU.is_equal))
            seen(inverted)
            normal = step(dve.tensor_scalar(wn[:, 0, :], top[:, 0:K], topsum[:, 1:2], None, ALU.mult))
            seen(marked)
            dve.tensor_tensor(chosen[:], hot[:, 0, :], hot[:, 1, :], ALU.add).then_inc(chosen_ready, 1)
            seen(normal)
            scale = 1.0 / NUM_MOE_LAYERS
            partly = step(dve.tensor_scalar(wn[:, 1, :], wn[:, 0, :], 1.0 - scale, None, ALU.mult))

            def split_shared(k):
                dve.wait_ge(sh_hi_done, k + 1)
                c = slice(k * CH, (k + 1) * CH)
                dve.tensor_tensor(sh_lo[:, c], w_raw[1][:, c], sh_hi[:, c].bitcast(f32), ALU.subtract
                                  ).then_inc(sh_lo_done, 1)

            split_shared(0)
            dve.wait_ge(x_hi_done, 1)
            dve.tensor_tensor(x_hl[:, 0:T, 1, :], acc[:, 0:N].rearrange("p (b s) -> p b s", s=S),
                              x_hl[:, 0:T, 0, :].bitcast(f32), ALU.subtract).then_inc(x0_lo_done, 1)
            dve.wait_ge(counts_done, 1)
            compared = step(dve.tensor_tensor(
                more[:], HB[:, E:2 * E].unsqueeze(2).to_broadcast([P, E, E]),
                const_sb[:, C_K16:C_TRI8].unsqueeze(1).to_broadcast([P, E, E]), ALU.is_gt))
            seen(partly)
            mixed = step(dve.scalar_tensor_tensor(wn[:, 2, :], wn[:, 0, :], scale, wn[:, 1, :], ALU.mult, ALU.add))
            seen(compared)
            counted = step(dve.reduce_sum(tiles_of[:], more[:], AX.X))
            seen(mixed)
            w_all = wn[:, 2, :].unsqueeze(2).to_broadcast([P, K, P])
            spread = step(dve.tensor_copy(w_rep[:, 0], w_all))
            seen(counted)
            masked = step(dve.tensor_tensor(
                before[:], const_sb[:, C_TRI8:C_B].rearrange("p (e f) -> p e f", f=E),
                tiles_of[:].unsqueeze(1).to_broadcast([P, E, E]), ALU.mult))
            split_shared(1)
            seen(masked)
            started = step(dve.reduce_sum(start[:], before[:], AX.X))
            seen(spread)
            dve.tensor_tensor(w_rep[:, 1], w_all, w_rep[:, 0].bitcast(f32), ALU.subtract).then_inc(rep_ready, 1)
            seen(started)
            seen(step(dve.scalar_tensor_tensor(place[:], start[:], float(T), HB[:, 0:E], ALU.mult, ALU.add)))
            seen(step(dve.tensor_tensor(place_k[:], hot[:], place[:].unsqueeze(1).to_broadcast([P, K, E]), ALU.mult)))
            placed = step(dve.reduce_sum(pos[:], place_k[:], AX.X))
            split_shared(2)
            seen(placed)
            for k in range(K):
                dve.tensor_scalar(at_slot[:, k, :], const_sb[:, C_IOTA:C_K16], pos[:, k:k + 1], None, ALU.is_equal)
            dve.tensor_copy(pos_rep[:], pos[:].unsqueeze(2).to_broadcast([P, K, P])).then_inc(slots_ready, 1)
            seen(step(dve.tensor_tensor(
                past[:], const_sb[0:1, C_IOTA:C_IOTA + UNITS].unsqueeze(2).to_broadcast([1, UNITS, E - 1]),
                start[0:1, 1:E].unsqueeze(1).to_broadcast([1, UNITS, E - 1]), ALU.is_ge)))
            seen(step(dve.reduce_sum(expert_f[:], past[:], AX.X)))
            dve.tensor_copy(expert_i[:, 0:UNITS], expert_f[:]).then_inc(expert_ready, 1)

            def slot_tables():
                dve.wait_ge(tables_done, 1)
                dve.tensor_scalar(slot_i[:], HB[0:1, 0:SLOTS], float(2 * S), None, ALU.mult)
                dve.tensor_scalar(pos_i[:].rearrange("p b k -> p k b"),
                                  D[1][0:1, 0:K * B].rearrange("p (k b) -> p k b", k=K),
                                  float(S), None, ALU.mult).then_inc(tables_ready, 1)
                dve.tensor_copy(w_slot[:], OB[:, 0:SLOTS]).then_inc(dve_step, 1)

            def split_weights(r, par, k):
                dve.wait_ge(whi_done, NC * r + k + 1)
                c = slice(k * CH, (k + 1) * CH)
                dve.tensor_tensor(w_lo[par][:, c], w_raw[par][:, c], w_hi[par][:, c].bitcast(f32),
                                  ALU.subtract).then_inc(wlo_done, 1)

            def unit(v, par, between=(), after_step=()):
                for j in range(NB):
                    q = NB * v + j
                    dve.wait_ge(gelu_done, q + 1)
                    dve.wait_ge(up_done, q + 1)
                    dve.tensor_tensor(U[j % 2][:], g[j % 2][:], U[j % 2][:], ALU.mult).then_inc(mul_done, 1)
                    for k, f, args in between:
                        if k == j:
                            f(*args)
                    dve.wait_ge(ahi_done, q + 1)
                    dve.tensor_tensor(a_lo[j][:], U[j % 2][:], a_hi[j][:].bitcast(f32), ALU.subtract
                                      ).then_inc(alo_done, 1)
                    for k, f, args in after_step:
                        if k == j:
                            f(*args)

            def finish_routed(v, par, r):
                dve.wait_ge(down_done, v + 1)
                dve.tensor_tensor(y[:, cols(r)].rearrange("p (b s) -> p b s", s=S),
                                  D[par][:].rearrange("p (b s) -> p b s", s=S),
                                  w_slot[:, ds(r * T, T)].unsqueeze(2).to_broadcast([P, T, S]),
                                  ALU.mult).then_inc(y_done, 1)

            def finish_shared(v, par, t):
                dve.wait_ge(down_done, v + 1)
                if not (isinstance(v, int) and v < FIRST):
                    dve.wait_ge(pairs_added, TILES if t == TILES - 1 else t - FIRST + 1)
                dve.tensor_tensor(acc[:, cols(t)], D[par][:], acc[:, cols(t)], ALU.add).then_inc(y_done, 1)

            def split_z(n, t, out, z_high):
                dve.wait_ge(zhi_done, n + 1)
                dve.tensor_tensor(out, acc[:, cols(t)], z_high.bitcast(f32), ALU.subtract
                                  ).then_inc(zlo_done, 1)

            def weigh_h(n, t, h_bank):
                dve.wait_ge(h_done, n + 1)
                dve.tensor_tensor(h_bank[:].rearrange("p (b s) -> p b s", s=S),
                                  h_bank[:].rearrange("p (b s) -> p b s", s=S),
                                  cond_er[:, ds(t * T, T)].unsqueeze(2).to_broadcast([P, T, S]),
                                  ALU.mult).then_inc(hw_done, 1)

            def split_h(n, out, h_high, h_bank):
                dve.wait_ge(hhi_done, n + 1)
                dve.tensor_tensor(out, h_bank[:], h_high.bitcast(f32), ALU.subtract).then_inc(hlo_done, 1)

            def split_steps(r, par):
                return [(k, split_weights, (r, par, k)) for k in range(NC)]

            def routed(v, par, before=finish_routed):
                t = v - 1 - (FIRST if before is finish_routed else 0)
                unit(v, par, split_steps(v + 1 - FIRST, 1 - par) + [(3, before, (v - 1, 1 - par, t))])

            unit(0, 0)
            slot_tables()
            routed(1, 1, finish_shared)
            seen(count[0] + 1)
            routed(2, 0, finish_shared)
            with dve.Fori(3, 22, 2) as v:
                routed(v, 1)
                routed(v + 1, 0)
            routed(23, 1)
            dve.wait_ge(lora_in, 16)
            dve.tensor_tensor(lora_raw[:, P:2 * P], lora_raw[:, P:2 * P], const_sb[:, C_ID:C_ONE], ALU.add
                              ).then_inc(lora_ready, 1)
            dve.wait_ge(lora_hi_done, 1)
            dve.tensor_tensor(lora_lo[:], lora_raw[:], lora_hi[:].bitcast(f32), ALU.subtract).then_inc(lora_split, 1)
            dve.wait_ge(cond_er_in, 16 * R)
            dve.tensor_scalar(cond_er[:], cond_er[:], LORA_SCALE, None, ALU.mult).then_inc(dve_step, 1)
            unit(24, 0, [(1, finish_routed, (23, 1, 21))])
            unit(25, 1, [(1, finish_routed, (24, 0, 22))])
            seen(count[0] + 2)

            def lora_steps(v, par):
                n, t = v - 26, v - 24
                before = [(0, split_h, (n - 1, h_lo[:], h_hi[:], HB))] if n > 0 else []
                return dict(
                    between=before + [(1, finish_shared, (v - 1, 1 - par, t)),
                                      (2, split_z, (n, t, z_lo[par][:], z_hi[par][:]))],
                    after_step=[(3, weigh_h, (n, t, HB))])

            for v in range(26, 30):
                unit(v, v % 2, **lora_steps(v, v % 2))
            last = lora_steps(30, 0)
            last["between"] += [(3, split_z, (6, 1, TAIL[6][0][1], TAIL[6][0][0]))]
            last["after_step"] = [(2, split_z, (5, 0, TAIL[5][0][1], TAIL[5][0][0])),
                                  *last["after_step"]]
            unit(30, 0, **last)
            finish_shared(30, 0, 7)
            split_h(4, h_lo[:], h_hi[:], HB)
            weigh_h(5, 0, TAIL[5][1][0])
            split_z(7, 7, TAIL[7][0][1], TAIL[7][0][0])
            weigh_h(6, 1, TAIL[6][1][0])
            split_h(5, TAIL[5][2][1], TAIL[5][2][0], TAIL[5][1][0])
            weigh_h(7, 7, TAIL[7][1][0])
            split_h(6, TAIL[6][2][1], TAIL[6][2][0], TAIL[6][1][0])
            split_h(7, TAIL[7][2][1], TAIL[7][2][0], TAIL[7][1][0])

        @block.gpsimd
        def _(pool):
            pool.wait_ge(const_in, 16)
            pool.tensor_copy(b_rep[:], const_sb[:, C_B:C_B + 1].to_broadcast([P, P]))
            pool.tensor_copy(ident[:], const_sb[:, C_ID:C_ONE]).then_inc(rep_ready, 1)
            for t in range(1, TILES):
                pool.wait_ge(x_hi_done, t + 1)
                pool.tensor_tensor(x_hl[:, t * T:(t + 1) * T, 1, :],
                                   acc[:, t * N:(t + 1) * N].rearrange("p (b s) -> p b s", s=S),
                                   x_hl[:, t * T:(t + 1) * T, 0, :].bitcast(f32), ALU.subtract
                                   ).then_inc(x_lo_done, 1)
            pool.wait_ge(tables_ready, 1)
            pool.wait_ge(x0_lo_done, 1)
            pool.wait_ge(x_lo_done, TILES - 1)

            def gather(r, par, early=False):
                if not early:
                    pool.wait_ge(up_done, NB * (r + FIRST - 1))
                _, rows = nc.values_load_multi_w_load_instructions(
                    slot_i[0:1, ds(r * T, T)], engines=[ENG.Pool], min_val=0, max_val=(B - 1) * 2 * S,
                    skip_runtime_bounds_check_because="the slots hold 64 times a batch row's number")
                flat = x_hl[:].rearrange("p b k s -> p (b k s)")
                for i in range(T):
                    last = pool.tensor_copy(xg[par][:, :, i * S:(i + 1) * S],
                                            flat[:, ds(rows[i], 2 * S)].rearrange("p (k s) -> p k s", s=S))
                last.then_inc(gathered, 1)

            gather(0, 0, early=True)
            gather(1, 1, early=True)
            with pool.Fori(2, UNITS - 2, 2) as r:
                gather(r, 0)
                gather(r + 1, 1)
            gather(UNITS - 1, (UNITS - 1) % 2)

            def combine(t, before):
                flat = pos_i[:].rearrange("p b k -> p (b k)")
                for h in range(2):
                    _, at = nc.values_load_multi_w_load_instructions(
                        flat[0:1, ds(t * K * T + h * T, T)], engines=[ENG.Pool],
                        min_val=0, max_val=(SLOTS - 1) * S,
                        skip_runtime_bounds_check_because="the positions are 32 times a slot's number")
                    if h == 0:
                        pool.wait_ge(y_done, FIRST + UNITS)
                    for i in range(T // 2):
                        c = (h * T // 2 + i) * S
                        last = pool.tensor_tensor(pair[:, c:c + S], y[:, ds(at[2 * i], S)],
                                                  y[:, ds(at[2 * i + 1], S)], ALU.add)
                last.then_inc(pair_done, 1)
                pool.wait_ge(pair_done, before + 1)
                pool.tensor_tensor(acc[:, cols(t)], acc[:, cols(t)], pair, ALU.add
                                   ).then_inc(pairs_added, 1)
                pool.wait_ge(pairs_added, before + 1)

            with pool.Fori(FIRST, TILES - 1) as t:
                combine(t, t - FIRST)
            with pool.Fori(0, FIRST) as t:
                combine(t, t + LAST - 1)
            combine(TILES - 1, TILES - 1)


_OUT = "out_dram"


def kernel(**inputs):
    import concourse.bacc as bacc
    from concourse.bass_utils import run_bass_kernel_spmd

    x = np.asarray(inputs["x"])
    cond = np.asarray(inputs["cond_8"])

    def packed(gate, up, down):
        lead = gate.shape[:-2]
        gate = gate.reshape(*lead, H, NB, 1, P)
        up = up.reshape(*lead, H, NB, 1, P)
        both = np.concatenate([gate, up], axis=-2).reshape(*lead, H, GU)
        down = np.moveaxis(down.reshape(*lead, NB, P, H), -3, -2).reshape(*lead, P, NB * H)
        return np.ascontiguousarray(np.concatenate([both, down], axis=-1))

    a = {n: np.asarray(v) for n, v in inputs.items()}
    arrays = {
        "xT": np.ascontiguousarray(x.reshape(B * S, H).T),
        "cond": np.ascontiguousarray(cond),
        "condT": np.ascontiguousarray(cond.T),
        "skill_w": packed(a["L0_cond_skill_gate"], a["L0_cond_skill_up"], a["L0_cond_skill_down"]),
        "shared_w": packed(a["L0_cond_shared_gate"], a["L0_cond_shared_up"], a["L0_cond_shared_down"]),
        "lora_w": np.ascontiguousarray(np.concatenate([
            a["L1_cond_As"].reshape(E * R, H).T,
            a["L1_cond_W_base"].T,
            a["L1_cond_Bs"].transpose(0, 2, 1).reshape(E * R, H)], axis=1)),
        "bias": np.ascontiguousarray(a["L1_cond_b_base"].reshape(H, 1)),
        "const": constants(),
    }
    nc = bacc.Bacc("TRN2", target_bir_lowering=False, num_devices=1)
    aps = {n: nc.dram_tensor(n, v.shape, mybir.dt.from_np(v.dtype), kind="ExternalInput").ap()
           for n, v in arrays.items()}
    outT = nc.dram_tensor(_OUT, (H, B * S), mybir.dt.float32, kind="ExternalOutput").ap()
    moe_lora_kernel(nc, **aps, outT=outT)
    result = run_bass_kernel_spmd(nc, [arrays], core_ids=[0]).results[0][_OUT]
    return np.ascontiguousarray(np.asarray(result).T).reshape(B, S, H)
```

```python
from contextlib import ExitStack

import numpy as np

import concourse.bass as bass
from concourse import mybir

P = 128
B, S, H, I = 128, 32, 128, 512
E, K = 8, 2
R, LORA_SCALE = 16, 2.0
NUM_MOE_LAYERS = 12
T = 16
N = T * S
TILES = B // T
FULL = K * B // T
HALF = E - 1
UNITS = HALF + FULL
SLOTS = T * FULL + T // 2 * HALF
NB = I // P
FIRST = 2
LAST = TILES - FIRST
ALL = TILES + UNITS
MIXED = 2 * HALF
LATE = FIRST + MIXED
AFTER = FIRST + UNITS
FINAL = ALL - 1
GU = 2 * I
WC = GU + NB * H
X_EARLY = 4
NC = 3
CH = WC // NC

C_TRI, C_ONE, C_STEP, C_TRI8, C_B, C_TILE, C_OWN, C_IOTA, C_ID, C_END = np.cumsum(
    [0, P, P, B // (T // 2), E * E, 1, UNITS, UNITS, SLOTS, P]).tolist()
C_EARLY = C_IOTA + E


def constants():
    c = np.zeros((P, C_END), np.float32)
    i = np.arange(P)
    c[:, C_TRI:C_ONE] = i[:, None] < i[None, :]
    c[:, C_ID:C_END] = np.eye(P)
    c[:, C_ONE:C_STEP] = 1.0
    c[:, C_IOTA:C_ID] = np.arange(SLOTS)
    steps = T * np.arange(B // T)
    c[:, C_STEP:C_TRI8] = np.concatenate([steps, steps + T // 2])
    e = np.arange(E)
    c[:, C_TRI8:C_B] = (e[None, :] < e[:, None]).reshape(1, -1)
    c[:, C_B] = i
    h = np.arange(HALF)
    c[:, C_OWN:C_IOTA] = -1
    c[:, C_OWN:C_OWN + MIXED:2] = HALF - 1 - h
    c[:, C_TILE:C_TILE + MIXED:2] = FULL + h // 2
    c[:, C_TILE + 1:C_TILE + MIXED:2] = h
    c[:, C_TILE + MIXED:C_OWN] = np.arange(HALF, FULL)
    return c


def moe_lora_kernel(nc, xT, cond, condT, skill_w, shared_w, lora_w, bias, const, outT):
    f32, f32r = mybir.dt.float32, mybir.dt.float32r
    i32, u32 = mybir.dt.int32, mybir.dt.uint32
    ALU, ACT, AX = mybir.AluOpType, mybir.ActivationFunctionType, mybir.AxisListType
    ENG = mybir.EngineType
    ds = bass.ds

    with ExitStack() as ctx:
        def sb(name, shape, dt=f32):
            return ctx.enter_context(nc.sbuf_tensor(name, shape, dt))

        def bank(name):
            return ctx.enter_context(nc.psum_tensor(name, [P, N], f32))

        def sem(name):
            return ctx.enter_context(nc.semaphore(name))

        acc = sb("acc", [P, B * S])
        x_hl = sb("x_hl", [P, B, 2, S], f32r)
        y = sb("y", [P, SLOTS * S])
        w_raw = [sb(f"w_raw{i}", [P, WC]) for i in range(2)]
        w_hi = [sb(f"w_hi{i}", [P, WC], f32r) for i in range(2)]
        w_lo = [sb(f"w_lo{i}", [P, WC], f32r) for i in range(2)]
        sh_hi = sb("sh_hi", [P, WC], f32r)
        sh_lo = sb("sh_lo", [P, WC], f32r)
        xg = [sb(f"xg{i}", [P, 2, N], f32r) for i in range(2)]
        xg_half = sb("xg_half", [P, 2, N // 2], f32r)
        g = [sb(f"g{i}", [P, N]) for i in range(NB)]
        a_hi = [sb(f"a_hi{j}", [P, N], f32r) for j in range(NB)]
        a_lo = [sb(f"a_lo{j}", [P, N], f32r) for j in range(NB)]
        lora_raw = sb("lora_raw", [P, 3 * P])
        lora_hi = sb("lora_hi", [P, 3 * P], f32r)
        lora_lo = sb("lora_lo", [P, 3 * P], f32r)
        bias_sb = sb("bias_sb", [P, 1])
        cond_er = sb("cond_er", [P, B])
        z_hi = [sb(f"z_hi{i}", [P, N], f32r) for i in range(2)]
        z_lo = [sb(f"z_lo{i}", [P, N], f32r) for i in range(2)]
        h_hi = sb("h_hi", [P, N], f32r)
        h_lo = sb("h_lo", [P, N], f32r)
        pair, *out_sb = (w[:, i * N:(i + 1) * N] for w in w_raw for i in range(3))
        OUTS = len(out_sb)
        const_sb = sb("const_sb", [P, C_END])
        logits = sb("logits", [P, E])
        negmax = sb("negmax", [P, 2])
        expd = sb("expd", [P, E])
        expsum = sb("expsum", [P, 2])
        gelu_unused = sb("gelu_unused", [P, 1])
        probs = sb("probs", [P, E])
        top = sb("top", [P, 8])
        top_i = sb("top_i", [P, 8], u32)
        top_f = sb("top_f", [P, K])
        hot = sb("hot", [P, K, E])
        chosen = sb("chosen", [P, E])
        topsum = sb("topsum", [P, 2])
        wn = sb("wn", [P, 3, K])
        w_rep = sb("w_rep", [P, 2, K, P], f32r)
        b_rep = sb("b_rep", [P, P], f32r)
        pos_rep = sb("pos_rep", [P, K, P], f32r)
        ident = sb("ident", [P, P], f32r)
        more = sb("more", [P, E, B // (T // 2)])
        counts = sb("counts", [P, E, 2])
        odd = sb("odd", [P, E])
        before = sb("before", [P, 2, E, E])
        odd_before = sb("odd_before", [P, E])
        halves = sb("halves", [P, E])
        fulls = sb("fulls", [P, E])
        start = sb("start", [P, E])
        rest = sb("rest", [P, E])
        in_half = sb("in_half", [P, E])
        at_full = sb("at_full", [P, E])
        at_half = sb("at_half", [P, E])
        apart = sb("apart", [P, E])
        moved = sb("moved", [P, E])
        place = sb("place", [P, E])
        place_k = sb("place_k", [P, K, E])
        pos = sb("pos", [P, K])
        own = sb("own", [1, UNITS, E])
        owner = sb("owner", [1, E])
        past = sb("past", [1, UNITS, 2 * E - 1])
        expert_f = sb("expert_f", [1, UNITS])
        at_slot = sb("at_slot", [P, K, SLOTS], f32r)
        w_slot = sb("w_slot", [P, SLOTS])
        expert_i = sb("expert_i", [1, 32], i32)
        slot_i = sb("slot_i", [1, SLOTS], i32)
        pos_i = sb("pos_i", [1, B, K], i32)

        G = [bank("G0"), bank("G1")]
        U = [bank("U0"), bank("U1")]
        D = [bank("D0"), bank("D1")]
        HB, OB = bank("HB"), bank("OB")

        cond_in, const_in, const_rest_in = sem("cond_in"), sem("const_in"), sem("const_rest_in")
        x0_in, shared_in = sem("x0_in"), [sem(f"shared{k}_in") for k in range(NC)]
        x_in = [sem(f"x{t}_in") for t in range(1, TILES)]
        lora_in, bias_in, cond_er_in = sem("lora_in"), sem("bias_in"), sem("cond_er_in")
        raw_in = [sem("raw0_in"), sem("raw1_in")]
        negmax_ready, exp_done = sem("negmax_ready"), sem("exp_done")
        chosen_ready, counts_done = sem("chosen_ready"), sem("counts_done")
        weights_ready, w_rep_done, rep_ready = sem("weights_ready"), sem("w_rep_done"), sem("rep_ready")
        expert_ready, slots_ready = sem("expert_ready"), sem("slots_ready")
        tables_done, tables_ready = sem("tables_done"), sem("tables_ready")
        sh_hi_done, sh_lo_done = sem("sh_hi_done"), [sem(f"sh_lo{k}_done") for k in range(NC)]
        x_hi_done, x0_lo_done, x_lo_done = sem("x_hi_done"), sem("x0_lo_done"), sem("x_lo_done")
        x_last_lo_done = sem("x_last_lo_done")
        lora_ready, lora_hi_done, lora_split = sem("lora_ready"), sem("lora_hi_done"), sem("lora_split")
        whi_done, gate_up_lo_done = sem("whi_done"), sem("gate_up_lo_done")
        full_down_lo_done, half_down_lo_done = sem("full_down_lo_done"), sem("half_down_lo_done")
        full_gathered, half_gathered = sem("full_gathered"), sem("half_gathered")
        gate_done, up_done, down_done = sem("gate_done"), sem("up_done"), sem("down_done")
        gelu_done, mul_done = sem("gelu_done"), sem("mul_done")
        ahi_done, alo_done = sem("ahi_done"), sem("alo_done")
        y_done = sem("y_done")
        pair_done, pairs_added = sem("pair_done"), sem("pairs_added")
        zhi_done, zlo_done = sem("zhi_done"), sem("zlo_done")
        h_done, hw_done = sem("h_done"), sem("hw_done")
        hhi_done, hlo_done = sem("hhi_done"), sem("hlo_done")
        o_done, out_ready = sem("o_done"), sem("out_ready")
        stored = [sem(f"stored{i}") for i in range(OUTS)]
        dve_step = sem("dve_step")

        block = ctx.enter_context(nc.Block())

        LORA_ORDER = [*range(FIRST, TILES - 1), 0, 1, TILES - 1]
        TAIL = {
            5: ((xg[0][:, 0, :], xg[0][:, 1, :]), G, (a_hi[2][:], a_lo[2][:])),
            6: ((xg[1][:, 0, :], xg[1][:, 1, :]), U, (a_hi[3][:], a_lo[3][:])),
            7: ((z_hi[1][:], z_lo[1][:]), (D[1], D[0]), (a_hi[0][:], a_lo[0][:])),
        }

        def cols(t, n=N):
            return ds(t * n, n)

        def rows(kind):
            return T // 2 if kind == "h" else T

        def steps_of(kind):
            return NB // 2 if kind == "h" else NB

        def first_step(v, kind):
            if kind == "h":
                return 3 * (v - FIRST) + NB * FIRST
            if kind == "m":
                return 3 * (v - FIRST - 1) + NB * FIRST + NB // 2
            if isinstance(v, int) and v < FIRST:
                return NB * v
            return NB * (v - LATE) + NB * FIRST + 3 * MIXED

        def number(v, kind):
            if kind == "f":
                return v - LATE + HALF + 1
            return half(v - FIRST) + 1

        def splits(kind):
            if kind == "h":
                return [(0, 1, 0), (1, 1, 1)]
            if kind == "m":
                return [(0, 0, 2), (1, 1, 0), (2, 1, 1), (3, 1, 2)]
            return [(0, 1, 0), (1, 1, 1), (2, 1, 2)]

        def first_slot(v, kind):
            if kind == "h":
                return (v - FIRST) * (T // 4) + FULL * T
            if kind == "m":
                return (v - FIRST - 1) * (T // 2)
            return (v - LATE + HALF) * T

        def half(r):
            return r // 2 if isinstance(r, int) else r >> 1

        @block.sync
        def _(sp):
            sp.dma_start(logits[:], cond).then_inc(cond_in, 16)

            def load_shared(k):
                c = slice(k * CH, (k + 1) * CH)
                sp.dma_start(w_raw[1][:, c], shared_w[:, c]).then_inc(shared_in[k], 16)

            sp.dma_start(const_sb[:, 0:C_EARLY], const[:, 0:C_EARLY]).then_inc(const_in, 16)
            load_shared(0)
            sp.dma_start(acc[:, 0:N], xT[:, 0:N]).then_inc(x0_in, 16)
            load_shared(1)
            sp.dma_start(const_sb[:, C_EARLY:], const[:, C_EARLY:]).then_inc(const_rest_in, 16)
            load_shared(2)
            for t in range(1, TILES):
                sp.dma_start(acc[:, t * N:(t + 1) * N], xT[:, t * N:(t + 1) * N]).then_inc(x_in[t - 1], 16)

            def fetch(v, par, before=None):
                e = sp.value_load(expert_i[0:1, ds(v - FIRST, 1)], min_val=0, max_val=E - 1)
                if before == "h":
                    sp.wait_ge(half_down_lo_done, number(v - 2, before))
                elif before is not None:
                    sp.wait_ge(full_down_lo_done, number(v - 2, before))
                sp.dma_start(w_raw[par][:], skill_w[ds(e, 1)].rearrange("e p c -> p (e c)")
                             ).then_inc(raw_in[par], 16)

            sp.wait_ge(expert_ready, 1)
            fetch(FIRST, 0)
            sp.wait_ge(sh_hi_done, NC)
            for k in range(NC):
                sp.wait_ge(sh_lo_done[k], 1)
            fetch(FIRST + 1, 1)
            sp.dma_start(lora_raw[:], lora_w).then_inc(lora_in, 16)
            sp.dma_start(bias_sb[:], bias).then_inc(bias_in, 16)
            for r in range(R):
                sp.dma_start(cond_er[r:P:R, :], condT).then_inc(cond_er_in, 16)
            with sp.Fori(FIRST + 2, LATE - 1, 2) as v:
                fetch(v, 0, "h")
                fetch(v + 1, 1, "m")
            fetch(LATE, 0, "h")
            fetch(LATE + 1, 1, "m")
            with sp.Fori(LATE + 2, AFTER - 2, 2) as v:
                fetch(v, 0, "f")
                fetch(v + 1, 1, "f")
            fetch(AFTER - 1, 0, "f")

            for n, t in enumerate(LORA_ORDER):
                sp.wait_ge(out_ready, n + 1)
                sp.dma_start(outT[:, t * N:(t + 1) * N], out_sb[n % OUTS]).then_inc(stored[n % OUTS], 16)
            for i in range(OUTS):
                sp.wait_ge(stored[i], 16 * len(range(i, TILES, OUTS)))

        @block.tensor
        def _(pe):
            def product(out, lhs, rhs, start, stop):
                pe.matmul(out, lhs[0], rhs[0], start=start, stop=False)
                pe.matmul(out, lhs[0], rhs[1], start=False, stop=False)
                return pe.matmul(out, lhs[1], rhs[0], start=False, stop=stop)

            def down(v, par, kind, ring, j, w):
                if j == 0:
                    if not (isinstance(v, int) and v < 2):
                        pe.wait_ge(y_done, v - 1)
                    if kind != "s":
                        pe.wait_ge(half_down_lo_done if kind == "h" else full_down_lo_done, number(v, kind))
                    elif isinstance(v, int) and v == 0:
                        pe.wait_ge(sh_lo_done[2], 1)
                    elif isinstance(v, int) and v == 1:
                        pe.wait_ge(tables_ready, 1)
                pe.wait_ge(alo_done, first_step(v, kind) + j + 1)
                blocks, n = NB // steps_of(kind), rows(kind) * S
                for i in range(blocks):
                    b = blocks * j + i
                    c = slice(GU + b * H, GU + (b + 1) * H)
                    a = (ring + j) % NB
                    last = product(D[par][:, 0:n], (w[0][:, c], w[1][:, c]),
                                   (a_hi[a][:, i * n:(i + 1) * n], a_lo[a][:, i * n:(i + 1) * n]),
                                   start=b == 0, stop=b == NB - 1)
                if b == NB - 1:
                    last.then_inc(down_done, 1)

            def steps(v, par, this, before, ring, t=None, buf=None):
                w = (sh_hi, sh_lo) if this == "s" else (w_hi[par], w_lo[par])
                w_before = (sh_hi, sh_lo) if before == "s" else (w_hi[1 - par], w_lo[1 - par])
                blocks, n = NB // steps_of(this), rows(this) * S
                if this != "s":
                    r = v - FIRST
                    x = xg_half if this == "h" else xg[buf]
                    rhs = (x[:, 0, :], x[:, 1, :])
                    pe.wait_ge(half_gathered if this == "h" else full_gathered, number(v, this))
                else:
                    rhs = tuple(x_hl[:, ds(t * T, T), k, :] for k in range(2))
                for j in range(steps_of(this)):
                    q = first_step(v, this) + j
                    first = isinstance(v, int) and q < 2
                    if blocks * j % 2 == 0 and this != "s":
                        pe.wait_ge(gate_up_lo_done, 2 * r + 1 + blocks * j // 2)
                    if j % 2 == 0 and isinstance(v, int) and v == 0:
                        pe.wait_ge(sh_lo_done[j // 2], 1)
                    if not first:
                        pe.wait_ge(gelu_done, q - 1)
                    for i in range(blocks):
                        c = 2 * (blocks * j + i) * P
                        last = product(G[j % 2][:, i * n:(i + 1) * n], (w[0][:, c:c + P], w[1][:, c:c + P]),
                                       rhs, True, True)
                    last.then_inc(gate_done, 1)
                    if not first:
                        pe.wait_ge(mul_done, q - 1)
                    for i in range(blocks):
                        c = 2 * (blocks * j + i) * P + P
                        last = product(U[j % 2][:, i * n:(i + 1) * n], (w[0][:, c:c + P], w[1][:, c:c + P]),
                                       rhs, True, True)
                    last.then_inc(up_done, 1)
                    if j >= 2:
                        down(v, par, this, ring, j - 2, w)
                    elif before is not None:
                        k = steps_of(before)
                        down(v - 1, 1 - par, before, (ring - k) % NB, k - 2 + j, w_before)
                    yield j

            def unit(*args, **kinds):
                for _ in steps(*args, **kinds):
                    pass

            lora = [(lora_hi[:, k * P:(k + 1) * P], lora_lo[:, k * P:(k + 1) * P]) for k in range(3)]

            def lora_in_products(n, z, banks, reused=False):
                pe.wait_ge(zlo_done, n + 1)
                if reused:
                    pe.wait_ge(hlo_done, n)
                    pe.wait_ge(out_ready, n)
                product(banks[0][:], lora[0], z, True, True).then_inc(h_done, 1)
                product(banks[1][:], lora[1], z, True, False)

            def lora_out_product(n, h, banks):
                pe.wait_ge(hlo_done, n + 1)
                product(banks[1][:], lora[2], h, False, True).then_inc(o_done, 1)

            pe.wait_ge(const_in, 16)
            pe.wait_ge(chosen_ready, 1)
            pe.matmul(HB[:, 0:E], const_sb[:, C_TRI:C_ONE], chosen[:], start=True, stop=True)
            pe.matmul(HB[:, E:2 * E], const_sb[:, C_ONE:C_STEP], chosen[:], start=True, stop=True
                      ).then_inc(counts_done, 1)

            def table_products():
                pe.wait_ge(slots_ready, 1)
                pe.wait_ge(rep_ready, 1)
                for k in range(K):
                    for part in range(2):
                        pe.matmul(OB[:, 0:SLOTS], w_rep[:, part, k, :], at_slot[:, k, :],
                                  start=k + part == 0, stop=k + part == K)
                for k in range(K):
                    pe.matmul(HB[:, 0:SLOTS], b_rep[:], at_slot[:, k, :], start=k == 0, stop=k == K - 1)
                for k in range(K):
                    last = pe.matmul(D[1][:, k * B:(k + 1) * B], pos_rep[:, k, :], ident[:],
                                     start=True, stop=True)
                last.then_inc(tables_done, 1)

            pe.wait_ge(x_hi_done, 1)
            pe.wait_ge(x0_lo_done, 1)
            for j in steps(0, 0, "s", None, 0, t=0):
                if j == 1:
                    table_products()
            pe.wait_ge(x_hi_done, 2)
            pe.wait_ge(x_lo_done, 1)
            unit(1, 1, "s", "s", 0, t=1)
            unit(FIRST, 0, "h", "s", 0)
            with pe.Fori(FIRST + 1, LATE - 4, 4) as v:
                unit(v, 1, "m", "h", 2, buf=0)
                unit(v + 1, 0, "h", "m", 2)
                unit(v + 2, 1, "m", "h", 0, buf=1)
                unit(v + 3, 0, "h", "m", 0)
            unit(LATE - 1, 1, "m", "h", 2, buf=0)
            with pe.Fori(LATE, AFTER - 2, 2) as v:
                unit(v, 0, "f", "f", 2, buf=1)
                unit(v + 1, 1, "f", "f", 2, buf=0)
            unit(AFTER - 1, 0, "f", "f", 2, buf=1)
            unit(AFTER, 1, "s", "f", 2, t=FIRST)

            def shared_with_lora(v, par, start=False):
                n = v - AFTER - 1
                for j in steps(v, par, "s", "s", 2, t=v - UNITS):
                    if j == 1 and not start:
                        lora_out_product(n - 1, (h_hi[:], h_lo[:]), (HB, OB))
                    if j == 3:
                        lora_in_products(n, (z_hi[par][:], z_lo[par][:]), (HB, OB), not start)

            pe.wait_ge(lora_split, 1)
            shared_with_lora(AFTER + 1, 0, start=True)
            with pe.Fori(AFTER + 2, FINAL - 2, 2) as v:
                shared_with_lora(v, 1)
                shared_with_lora(v + 1, 0)
            shared_with_lora(FINAL - 1, 1)
            shared_with_lora(FINAL, 0)
            for j in (2, 3):
                down(FINAL, 0, "s", 2, j, (sh_hi, sh_lo))
            lora_in_products(5, *TAIL[5][0:2])
            lora_in_products(6, *TAIL[6][0:2])
            lora_in_products(7, *TAIL[7][0:2])
            lora_out_product(4, (h_hi[:], h_lo[:]), (HB, OB))
            for n in (5, 6, 7):
                lora_out_product(n, TAIL[n][2], TAIL[n][1])

        @block.scalar
        def _(act):
            act.wait_ge(negmax_ready, 1)
            act.activation(expd[:], logits[:], ACT.Exp, bias=negmax[:, 1:2], scale=1.0,
                           accum_out=expsum[:, 0:1]).then_inc(exp_done, 1)

            act.activation(gelu_unused[:], negmax[:, 1:2], ACT.Gelu_apprx_tanh)

            def split_x(t):
                act.wait_ge(x0_in if t == 0 else x_in[t - 1], 16)
                act.activation(x_hl[:, t * T:(t + 1) * T, 0, :],
                               acc[:, t * N:(t + 1) * N].rearrange("p (b s) -> p b s", s=S), ACT.Copy
                               ).then_inc(x_hi_done, 1)

            for k in range(NC):
                act.wait_ge(shared_in[k], 16)
                c = slice(k * CH, (k + 1) * CH)
                act.activation(sh_hi[:, c], w_raw[1][:, c], ACT.Copy).then_inc(sh_hi_done, 1)
                if k == 0:
                    split_x(0)
            for t in range(1, X_EARLY):
                split_x(t)

            def split_weights(v, par, k):
                if k == 0:
                    act.wait_ge(raw_in[par], 16 * half(v - FIRST) + 16)
                c = slice(k * CH, (k + 1) * CH)
                act.activation(w_hi[par][:, c], w_raw[par][:, c], ACT.Copy).then_inc(whi_done, 1)

            def high_part(q, a):
                act.wait_ge(mul_done, q + 1)
                act.activation(a_hi[a][:], g[a][:], ACT.Copy).then_inc(ahi_done, 1)

            def catch_up(v):
                high_part(first_step(v, "s") + NB - 1, 1)

            def steps(v, par, this="s", ring=2, nxt=False, caught_up=None):
                for j in range(steps_of(this)):
                    q = first_step(v, this) + j
                    first = isinstance(v, int) and q < 2
                    act.wait_ge(gate_done, q + 1)
                    if not (isinstance(v, int) and q < NB):
                        act.wait_ge(alo_done, q - NB + 1)
                    act.activation(g[(ring + j) % NB][:], G[j % 2][:], ACT.Gelu_apprx_tanh
                                   ).then_inc(gelu_done, 1)
                    if not (isinstance(v, int) and q == 0 or j == caught_up):
                        high_part(q - 1, (ring + j - 1) % NB)
                    for k, on, chunk in splits(this) if nxt else ():
                        if k == j:
                            split_weights(v + on, (par + on) % 2, chunk)
                    yield j

            def unit(*args, **kinds):
                for _ in steps(*args, **kinds):
                    pass

            def split_z(n, t, out, reused=False):
                if isinstance(t, int) and t < FIRST:
                    act.wait_ge(pairs_added, LAST + t)
                else:
                    act.wait_ge(y_done, t + UNITS + 1)
                if reused:
                    act.wait_ge(o_done, n - 1)
                act.activation(out, acc[:, cols(t)], ACT.Copy).then_inc(zhi_done, 1)

            def split_h(n, out, h_bank, reused=False):
                act.wait_ge(hw_done, n + 1)
                if reused:
                    act.wait_ge(o_done, n)
                act.activation(out, h_bank[:], ACT.Copy).then_inc(hhi_done, 1)

            def output(n, o_bank):
                act.wait_ge(o_done, n + 1)
                if n >= OUTS:
                    act.wait_ge(stored[n % OUTS], 16 * (n // OUTS))
                act.activation(out_sb[n % OUTS], o_bank[:], ACT.Identity, bias=bias_sb[:, 0:1], scale=1.0
                               ).then_inc(out_ready, 1)

            def tables():
                act.wait_ge(tables_done, 1)
                act.activation(slot_i[:], HB[0:1, 0:SLOTS], ACT.Copy, scale=float(2 * S))
                act.activation(pos_i[:].rearrange("p b k -> p k b"),
                               D[1][0:1, 0:K * B].rearrange("p (k b) -> p k b", k=K), ACT.Copy,
                               scale=float(S)).then_inc(tables_ready, 1)

            for j in steps(0, 0, ring=0, caught_up=1):
                for t in (X_EARLY + 2 * j, X_EARLY + 2 * j + 1):
                    if t < TILES:
                        split_x(t)
                if j == 0:
                    high_part(0, 0)
                if j == 2:
                    tables()
            unit(1, 1, ring=0, nxt=True)
            unit(FIRST, 0, "h", ring=0, nxt=True)
            with act.Fori(FIRST + 1, LATE - 4, 4) as v:
                unit(v, 1, "m", ring=2, nxt=True)
                unit(v + 1, 0, "h", ring=2, nxt=True)
                unit(v + 2, 1, "m", ring=0, nxt=True)
                unit(v + 3, 0, "h", ring=0, nxt=True)
            unit(LATE - 1, 1, "m", nxt=True)
            with act.Fori(LATE, AFTER - 2, 2) as v:
                unit(v, 0, "f", nxt=True)
                unit(v + 1, 1, "f", nxt=True)
            unit(AFTER - 1, 0, "f")
            for j in steps(AFTER, 1):
                if j == 0:
                    act.wait_ge(lora_ready, 1)
                    act.activation(lora_hi[:], lora_raw[:], ACT.Copy).then_inc(lora_hi_done, 1)
            act.wait_ge(bias_in, 16)
            catch_up(AFTER)
            for v in range(AFTER + 1, ALL):
                n = v - AFTER - 1
                for j in steps(v, v % 2, caught_up=0):
                    if j == 0 and n > 0:
                        split_h(n - 1, h_hi[:], HB, n > 1)
                    if j == 2:
                        split_z(n, v - UNITS - 1, z_hi[v % 2][:], n > 1)
                        if n > 0:
                            output(n - 1, OB)
                        if v == FINAL:
                            split_z(5, 0, TAIL[5][0][0])
                catch_up(v)
            split_z(6, 1, TAIL[6][0][0])
            split_h(4, h_hi[:], HB, True)
            split_z(7, 7, TAIL[7][0][0])
            for n in (5, 6, 7):
                split_h(n, TAIL[n][2][0], TAIL[n][1][0])
            output(4, OB)
            for n in (5, 6, 7):
                output(n, TAIL[n][1][1])

        @block.vector
        def _(dve):
            count = [0]

            def step(instruction):
                count[0] += 1
                instruction.then_inc(dve_step, 1)
                return count[0]

            def seen(n):
                dve.wait_ge(dve_step, n)

            dve.wait_ge(cond_in, 16)
            seen(step(dve.reduce_max(negmax[:, 0:1], logits[:], AX.X)))
            dve.tensor_scalar(negmax[:, 1:2], negmax[:, 0:1], -1.0, None, ALU.mult).then_inc(negmax_ready, 1)
            dve.wait_ge(exp_done, 1)
            seen(step(dve.reciprocal(expsum[:, 1:2], expsum[:, 0:1])))
            seen(step(dve.tensor_scalar(probs[:], expd[:], expsum[:, 1:2], None, ALU.mult)))
            seen(step(dve.max(top[:], probs[:])))
            found = step(dve.max_index(top_i[:], top[:], probs[:]))
            summed = step(dve.tensor_tensor(topsum[:, 0:1], top[:, 0:1], top[:, 1:2], ALU.add))
            seen(found)
            index = step(dve.tensor_copy(top_f[:], top_i[:, 0:K]))
            seen(summed)
            inverted = step(dve.reciprocal(topsum[:, 1:2], topsum[:, 0:1]))
            dve.wait_ge(const_in, 16)
            seen(index)
            marked = step(dve.tensor_tensor(
                hot[:], const_sb[:, C_IOTA:C_IOTA + E].unsqueeze(1).to_broadcast([P, K, E]),
                top_f[:].unsqueeze(2).to_broadcast([P, K, E]), ALU.is_equal))
            seen(inverted)
            normal = step(dve.tensor_scalar(wn[:, 0, :], top[:, 0:K], topsum[:, 1:2], None, ALU.mult))
            seen(marked)
            dve.tensor_tensor(chosen[:], hot[:, 0, :], hot[:, 1, :], ALU.add).then_inc(chosen_ready, 1)
            seen(normal)
            scale = 1.0 / NUM_MOE_LAYERS
            partly = step(dve.tensor_scalar(wn[:, 1, :], wn[:, 0, :], 1.0 - scale, None, ALU.mult))

            def split_shared(k):
                dve.wait_ge(sh_hi_done, k + 1)
                c = slice(k * CH, (k + 1) * CH)
                dve.tensor_tensor(sh_lo[:, c], w_raw[1][:, c], sh_hi[:, c].bitcast(f32), ALU.subtract
                                  ).then_inc(sh_lo_done[k], 1)

            split_shared(0)

            def split_x(t, done):
                dve.wait_ge(x_hi_done, t + 1)
                dve.tensor_tensor(x_hl[:, t * T:(t + 1) * T, 1, :],
                                  acc[:, t * N:(t + 1) * N].rearrange("p (b s) -> p b s", s=S),
                                  x_hl[:, t * T:(t + 1) * T, 0, :].bitcast(f32), ALU.subtract).then_inc(done, 1)

            split_x(0, x0_lo_done)
            rank, length = HB[:, 0:E], HB[:, E:2 * E]
            tri = const_sb[:, C_TRI8:C_B].rearrange("p (e f) -> p e f", f=E)
            dve.wait_ge(counts_done, 1)
            compared = step(dve.tensor_tensor(
                more[:], length.unsqueeze(2).to_broadcast([P, E, B // (T // 2)]),
                const_sb[:, C_STEP:C_TRI8].unsqueeze(1).to_broadcast([P, E, B // (T // 2)]), ALU.is_gt))
            seen(partly)
            dve.scalar_tensor_tensor(wn[:, 2, :], wn[:, 0, :], scale, wn[:, 1, :], ALU.mult, ALU.add
                                     ).then_inc(weights_ready, 1)
            seen(compared)
            counted = step(dve.reduce_sum(counts[:], more[:].rearrange("p e (c k) -> p e c k", c=2), AX.X))
            seen(counted)
            left = step(dve.tensor_tensor(odd[:], counts[:, :, 0], counts[:, :, 1], ALU.subtract))
            ranked = step(dve.scalar_tensor_tensor(rest[:], counts[:, :, 1], -float(T), rank, ALU.mult, ALU.add))
            seen(left)
            masked = step(dve.tensor_tensor(before[:, 0], tri, odd[:].unsqueeze(1).to_broadcast([P, E, E]), ALU.mult))
            seen(masked)
            ordered = step(dve.reduce_sum(odd_before[:], before[:, 0], AX.X))
            seen(ordered)
            halved = step(dve.scalar_tensor_tensor(halves[:], odd_before[:], float(HALF), odd[:], ALU.is_lt, ALU.mult))
            far = step(dve.scalar_tensor_tensor(at_half[:], odd_before[:], -float(T // 2), rest[:], ALU.mult, ALU.add))
            seen(halved)
            filled = step(dve.tensor_tensor(fulls[:], counts[:, :, 0], halves[:], ALU.subtract))
            inside = step(dve.scalar_tensor_tensor(in_half[:], rest[:], 0.0, halves[:], ALU.is_ge, ALU.mult))
            seen(filled)
            masked = step(dve.tensor_tensor(before[:, 1], tri, fulls[:].unsqueeze(1).to_broadcast([P, E, E]), ALU.mult))
            seen(masked)
            seen(step(dve.reduce_sum(start[:], before[:, 1], AX.X)))
            near = step(dve.scalar_tensor_tensor(at_full[:], start[:], float(T), rank, ALU.mult, ALU.add))
            seen(near)
            seen(step(dve.scalar_tensor_tensor(
                apart[:], at_half[:], float(SLOTS - T // 2), at_full[:], ALU.add, ALU.subtract)))
            seen(step(dve.tensor_tensor(moved[:], in_half[:], apart[:], ALU.mult)))
            seen(step(dve.tensor_tensor(place[:], at_full[:], moved[:], ALU.add)))
            seen(step(dve.tensor_tensor(place_k[:], hot[:], place[:].unsqueeze(1).to_broadcast([P, K, E]), ALU.mult)))
            placed = step(dve.reduce_sum(pos[:], place_k[:], AX.X))
            seen(placed)
            dve.wait_ge(const_rest_in, 16)
            for k in range(K):
                dve.tensor_scalar(at_slot[:, k, :], const_sb[:, C_IOTA:C_ID], pos[:, k:k + 1], None, ALU.is_equal)
            dve.tensor_copy(pos_rep[:], pos[:].unsqueeze(2).to_broadcast([P, K, P])).then_inc(slots_ready, 1)

            def experts(part):
                tables = (1, UNITS, E)
                if part == 0:
                    dve.tensor_tensor(
                        own[:], const_sb[0:1, C_OWN:C_IOTA].unsqueeze(2).to_broadcast(tables),
                        odd_before[0:1, :].unsqueeze(1).to_broadcast(tables), ALU.is_equal)
                    step(dve.scalar_tensor_tensor(
                        owner[:], const_sb[0:1, C_IOTA:C_IOTA + E], float(1 - E), halves[0:1, :], ALU.add, ALU.mult))
                    dve.tensor_tensor(
                        past[:, :, 0:E - 1], const_sb[0:1, C_TILE:C_OWN].unsqueeze(2).to_broadcast([1, UNITS, E - 1]),
                        start[0:1, 1:E].unsqueeze(1).to_broadcast([1, UNITS, E - 1]), ALU.is_ge)
                    return
                seen(count[0])
                seen(step(dve.tensor_tensor(
                    past[:, :, E - 1:], own[:], owner[:].unsqueeze(1).to_broadcast(tables), ALU.mult)))
                seen(step(dve.reduce_sum(expert_f[:], past[:], AX.X)))
                dve.tensor_copy(expert_i[:, 0:UNITS], expert_f[:]).then_inc(expert_ready, 1)

            def split_weights(v, par, k):
                dve.wait_ge(whi_done, NC * (v - FIRST) + k + 1)
                c = slice(k * CH, (k + 1) * CH)
                dve.tensor_tensor(w_lo[par][:, c], w_raw[par][:, c], w_hi[par][:, c].bitcast(f32),
                                  ALU.subtract).then_inc(full_down_lo_done if k == 2 else gate_up_lo_done, 1)

            def low_part(q, a):
                dve.wait_ge(ahi_done, q + 1)
                dve.tensor_tensor(a_lo[a][:], g[a][:], a_hi[a][:].bitcast(f32), ALU.subtract
                                  ).then_inc(alo_done, 1)

            def catch_up(v):
                low_part(first_step(v, "s") + NB - 1, 1)

            def steps(v, par, this="s", ring=2, caught_up=None):
                for j in range(steps_of(this)):
                    q = first_step(v, this) + j
                    a = (ring + j) % NB
                    dve.wait_ge(gelu_done, q + 1)
                    dve.wait_ge(up_done, q + 1)
                    dve.tensor_tensor(g[a][:], g[a][:], U[j % 2][:], ALU.mult).then_inc(mul_done, 1)
                    if not (isinstance(v, int) and q == 0 or j == caught_up):
                        low_part(q - 1, (ring + j - 1) % NB)
                    yield j

            def finish_routed(v, par, kind):
                m, slot = rows(kind), first_slot(v, kind)
                dve.wait_ge(down_done, v + 1)
                dve.tensor_tensor(y[:, ds(slot * S, m * S)].rearrange("p (b s) -> p b s", s=S),
                                  D[par][:, 0:m * S].rearrange("p (b s) -> p b s", s=S),
                                  w_slot[:, ds(slot, m)].unsqueeze(2).to_broadcast([P, m, S]),
                                  ALU.mult).then_inc(y_done, 1)

            def finish_shared(v, par, t):
                dve.wait_ge(down_done, v + 1)
                if not (isinstance(v, int) and v < FIRST):
                    dve.wait_ge(pairs_added, TILES if t == TILES - 1 else t - FIRST + 1)
                dve.tensor_tensor(acc[:, cols(t)], D[par][:], acc[:, cols(t)], ALU.add).then_inc(y_done, 1)

            def split_z(n, t, out, z_high):
                dve.wait_ge(zhi_done, n + 1)
                dve.tensor_tensor(out, acc[:, cols(t)], z_high.bitcast(f32), ALU.subtract
                                  ).then_inc(zlo_done, 1)

            def weigh_h(n, t, h_bank):
                dve.wait_ge(h_done, n + 1)
                dve.tensor_tensor(h_bank[:].rearrange("p (b s) -> p b s", s=S),
                                  h_bank[:].rearrange("p (b s) -> p b s", s=S),
                                  cond_er[:, ds(t * T, T)].unsqueeze(2).to_broadcast([P, T, S]),
                                  ALU.mult).then_inc(hw_done, 1)

            def split_h(n, out, h_high, h_bank):
                dve.wait_ge(hhi_done, n + 1)
                dve.tensor_tensor(out, h_bank[:], h_high.bitcast(f32), ALU.subtract).then_inc(hlo_done, 1)

            def split_in_step(v, par, this, nxt, j):
                for k, on, chunk in splits(this):
                    if k == j and not (nxt == "h" and on == 1 and chunk == 2):
                        split_weights(v + on, (par + on) % 2, chunk)

            def mixed(v, ring, nxt="h"):
                for j in steps(v, 1, "m", ring):
                    split_in_step(v, 1, "m", nxt, j)
                    if j == 3:
                        finish_routed(v - 1, 0, "h")

            def half_unit(v, ring):
                for j in steps(v, 0, "h", ring):
                    split_in_step(v, 0, "h", "m", j)
                    if j == 1 and isinstance(v, int) and v == FIRST:
                        finish_shared(1, 1, 1)
                    elif j == 1:
                        finish_routed(v - 1, 1, "m")

            def full(v, par, before="f"):
                for j in steps(v, par, "f"):
                    split_in_step(v, par, "f", "f", j)
                    if j == 3:
                        finish_routed(v - 1, 1 - par, before)

            for j in steps(0, 0, ring=0, caught_up=1):
                if j == 0:
                    experts(0)
                    low_part(0, 0)
                    experts(1)
                if j == 2:
                    split_x(TILES - 1, x_last_lo_done)
            dve.wait_ge(tables_done, 1)
            weighed = step(dve.tensor_copy(w_slot[:], OB[:, 0:SLOTS]))
            for j in steps(1, 1, ring=0):
                split_in_step(1, 1, "s", "h", j)
                if j == 3:
                    finish_shared(0, 0, 0)
            half_unit(FIRST, 0)
            seen(weighed)
            with dve.Fori(FIRST + 1, LATE - 4, 4) as v:
                mixed(v, 2)
                half_unit(v + 1, 2)
                mixed(v + 2, 0)
                half_unit(v + 3, 0)
            mixed(LATE - 1, 2, "f")
            full(LATE, 0, "m")
            with dve.Fori(LATE + 1, AFTER - 3, 2) as v:
                full(v, 1)
                full(v + 1, 0)
            full(AFTER - 2, 1)
            for j in steps(AFTER - 1, 0, "f"):
                if j == 1:
                    finish_routed(AFTER - 2, 1, "f")
                if j == 2:
                    dve.wait_ge(lora_in, 16)
                    dve.tensor_tensor(lora_raw[:, P:2 * P], lora_raw[:, P:2 * P], const_sb[:, C_ID:C_END],
                                      ALU.add).then_inc(lora_ready, 1)
                if j == 3:
                    dve.wait_ge(cond_er_in, 16 * R)
                    scaled = step(dve.tensor_scalar(cond_er[:], cond_er[:], LORA_SCALE, None, ALU.mult))
            for j in steps(AFTER, 1):
                if j == 1:
                    finish_routed(AFTER - 1, 0, "f")
                if j == 2:
                    dve.wait_ge(lora_hi_done, 1)
                    dve.tensor_tensor(lora_lo[:], lora_raw[:], lora_hi[:].bitcast(f32), ALU.subtract
                                      ).then_inc(lora_split, 1)
            catch_up(AFTER)
            seen(scaled)
            for v in range(AFTER + 1, ALL):
                n, t = v - AFTER - 1, v - UNITS - 1
                for j in steps(v, v % 2, caught_up=0):
                    if j == 0 and n > 0:
                        split_h(n - 1, h_lo[:], h_hi[:], HB)
                    if j == 1:
                        finish_shared(v - 1, 1 - v % 2, t)
                    if j == 2:
                        split_z(n, t, z_lo[v % 2][:], z_hi[v % 2][:])
                        if v == FINAL:
                            split_z(5, 0, TAIL[5][0][1], TAIL[5][0][0])
                    if j == 3 and v < FINAL:
                        weigh_h(n, t, HB)
                catch_up(v)
            weigh_h(4, 6, HB)
            split_z(6, 1, TAIL[6][0][1], TAIL[6][0][0])
            finish_shared(FINAL, 0, 7)
            split_h(4, h_lo[:], h_hi[:], HB)
            weigh_h(5, 0, TAIL[5][1][0])
            split_z(7, 7, TAIL[7][0][1], TAIL[7][0][0])
            weigh_h(6, 1, TAIL[6][1][0])
            split_h(5, TAIL[5][2][1], TAIL[5][2][0], TAIL[5][1][0])
            weigh_h(7, 7, TAIL[7][1][0])
            split_h(6, TAIL[6][2][1], TAIL[6][2][0], TAIL[6][1][0])
            split_h(7, TAIL[7][2][1], TAIL[7][2][0], TAIL[7][1][0])

        @block.gpsimd
        def _(pool):
            pool.wait_ge(const_in, 16)
            pool.tensor_copy(b_rep[:], const_sb[:, C_B:C_B + 1].to_broadcast([P, P]))

            def split_shared(k):
                c = slice(k * CH, (k + 1) * CH)
                pool.wait_ge(sh_hi_done, k + 1)
                pool.tensor_tensor(sh_lo[:, c], w_raw[1][:, c], sh_hi[:, c].bitcast(f32), ALU.subtract
                                   ).then_inc(sh_lo_done[k], 1)

            split_shared(1)
            pool.wait_ge(weights_ready, 1)
            w_all = wn[:, 2, :].unsqueeze(2).to_broadcast([P, K, P])
            pool.tensor_copy(w_rep[:, 0], w_all).then_inc(w_rep_done, 1)
            pool.wait_ge(const_rest_in, 16)
            pool.tensor_copy(ident[:], const_sb[:, C_ID:C_END])
            pool.wait_ge(w_rep_done, 1)
            pool.tensor_tensor(w_rep[:, 1], w_all, w_rep[:, 0].bitcast(f32), ALU.subtract).then_inc(rep_ready, 1)
            split_shared(2)
            for t in range(1, TILES - 1):
                pool.wait_ge(x_hi_done, t + 1)
                pool.tensor_tensor(x_hl[:, t * T:(t + 1) * T, 1, :],
                                   acc[:, t * N:(t + 1) * N].rearrange("p (b s) -> p b s", s=S),
                                   x_hl[:, t * T:(t + 1) * T, 0, :].bitcast(f32), ALU.subtract
                                   ).then_inc(x_lo_done, 1)
            pool.wait_ge(tables_ready, 1)
            pool.wait_ge(x0_lo_done, 1)
            pool.wait_ge(x_lo_done, TILES - 2)
            pool.wait_ge(x_last_lo_done, 1)

            def gather(v, kind, buf=None, after=None, its="m"):
                if after is not None:
                    its = "h" if kind == "h" else its
                    pool.wait_ge(up_done, first_step(after, its) + steps_of(its))
                _, row = nc.values_load_multi_w_load_instructions(
                    slot_i[0:1, ds(first_slot(v, kind), rows(kind))], engines=[ENG.Pool],
                    min_val=0, max_val=(B - 1) * 2 * S,
                    skip_runtime_bounds_check_because="the slots hold 64 times a batch row's number")
                flat = x_hl[:].rearrange("p b k s -> p (b k s)")
                x = xg_half if kind == "h" else xg[buf]
                for i in range(rows(kind)):
                    last = pool.tensor_copy(x[:, :, i * S:(i + 1) * S],
                                            flat[:, ds(row[i], 2 * S)].rearrange("p (k s) -> p k s", s=S))
                last.then_inc(half_gathered if kind == "h" else full_gathered, 1)

            def split_down(v):
                c = slice(2 * CH, 3 * CH)
                pool.wait_ge(whi_done, NC * (v - FIRST) + NC)
                pool.wait_ge(gate_up_lo_done, 2 * (v - FIRST) + 2)
                pool.tensor_tensor(w_lo[0][:, c], w_raw[0][:, c], w_hi[0][:, c].bitcast(f32),
                                   ALU.subtract).then_inc(half_down_lo_done, 1)

            gather(2, "h")
            gather(3, "m", 0)
            split_down(2)
            gather(5, "m", 1)
            gather(4, "h", after=2)
            split_down(4)
            with pool.Fori(7, LATE - 4, 4) as v:
                gather(v, "m", 0, after=v - 4)
                gather(v - 1, "h", after=v - 3)
                split_down(v - 1)
                gather(v + 2, "m", 1, after=v - 2)
                gather(v + 1, "h", after=v - 1)
                split_down(v + 1)
            gather(15, "m", 0, after=11)
            gather(14, "h", after=12)
            split_down(14)
            gather(16, "f", 1, after=13)
            gather(17, "f", 0, after=15)
            with pool.Fori(LATE + 2, AFTER - 2, 2) as v:
                gather(v, "f", 1, after=v - 2, its="f")
                gather(v + 1, "f", 0, after=v - 1, its="f")
            gather(AFTER - 1, "f", 1, after=AFTER - 3, its="f")

            def combine(t, before):
                flat = pos_i[:].rearrange("p b k -> p (b k)")
                for h in range(2):
                    _, at = nc.values_load_multi_w_load_instructions(
                        flat[0:1, ds(t * K * T + h * T, T)], engines=[ENG.Pool],
                        min_val=0, max_val=(SLOTS - 1) * S,
                        skip_runtime_bounds_check_because="the positions are 32 times a slot's number")
                    if h == 0:
                        pool.wait_ge(y_done, FIRST + UNITS)
                    for i in range(T // 2):
                        c = (h * T // 2 + i) * S
                        last = pool.tensor_tensor(pair[:, c:c + S], y[:, ds(at[2 * i], S)],
                                                  y[:, ds(at[2 * i + 1], S)], ALU.add)
                last.then_inc(pair_done, 1)
                pool.wait_ge(pair_done, before + 1)
                pool.tensor_tensor(acc[:, cols(t)], acc[:, cols(t)], pair, ALU.add
                                   ).then_inc(pairs_added, 1)
                pool.wait_ge(pairs_added, before + 1)

            with pool.Fori(FIRST, TILES - 1) as t:
                combine(t, t - FIRST)
            with pool.Fori(0, FIRST) as t:
                combine(t, t + LAST - 1)
            combine(TILES - 1, TILES - 1)


_OUT = "out_dram"


def kernel(**inputs):
    import concourse.bacc as bacc
    from concourse.bass_utils import run_bass_kernel_spmd

    x = np.asarray(inputs["x"])
    cond = np.asarray(inputs["cond_8"])

    def packed(gate, up, down):
        lead = gate.shape[:-2]
        gate = gate.reshape(*lead, H, NB, 1, P)
        up = up.reshape(*lead, H, NB, 1, P)
        both = np.concatenate([gate, up], axis=-2).reshape(*lead, H, GU)
        down = np.moveaxis(down.reshape(*lead, NB, P, H), -3, -2).reshape(*lead, P, NB * H)
        return np.ascontiguousarray(np.concatenate([both, down], axis=-1))

    a = {n: np.asarray(v) for n, v in inputs.items()}
    arrays = {
        "xT": np.ascontiguousarray(x.reshape(B * S, H).T),
        "cond": np.ascontiguousarray(cond),
        "condT": np.ascontiguousarray(cond.T),
        "skill_w": packed(a["L0_cond_skill_gate"], a["L0_cond_skill_up"], a["L0_cond_skill_down"]),
        "shared_w": packed(a["L0_cond_shared_gate"], a["L0_cond_shared_up"], a["L0_cond_shared_down"]),
        "lora_w": np.ascontiguousarray(np.concatenate([
            a["L1_cond_As"].reshape(E * R, H).T,
            a["L1_cond_W_base"].T,
            a["L1_cond_Bs"].transpose(0, 2, 1).reshape(E * R, H)], axis=1)),
        "bias": np.ascontiguousarray(a["L1_cond_b_base"].reshape(H, 1)),
        "const": constants(),
    }
    nc = bacc.Bacc("TRN2", target_bir_lowering=False, num_devices=1)
    aps = {n: nc.dram_tensor(n, v.shape, mybir.dt.from_np(v.dtype), kind="ExternalInput").ap()
           for n, v in arrays.items()}
    outT = nc.dram_tensor(_OUT, (H, B * S), mybir.dt.float32, kind="ExternalOutput").ap()
    moe_lora_kernel(nc, **aps, outT=outT)
    result = run_bass_kernel_spmd(nc, [arrays], core_ids=[0]).results[0][_OUT]
    return np.ascontiguousarray(np.asarray(result).T).reshape(B, S, H)
```
